# Optimizing a Trainium2 kernel written in Bass

```python
import numpy as np
import jax
import jax.numpy as jnp

def _softmax(x, axis=-1):
    return jax.nn.softmax(x, axis=axis)

def _gelu(x):
    return jax.nn.gelu(x, approximate=True)

def _silu(x):
    return jax.nn.silu(x)

def _sigmoid(x):
    return jax.nn.sigmoid(x)

def _layernorm(x, axis=-1, eps=1e-05):
    m = jnp.mean(x, axis=axis, keepdims=True)
    v = jnp.var(x, axis=axis, keepdims=True)
    return (x - m) / jnp.sqrt(v + eps)

def _scatter_add(tgt, idx, src, axis=0):
    return tgt.at[idx].add(src)

def _segment_sum(src, seg, n):
    return jax.ops.segment_sum(src, seg, n)
kernel_name = 'mk_flamingo_gated_d1_seqx_r4_ce8df3'

def setup_inputs(seed: int=0):
    np.random.seed(seed)
    _w = jnp.asarray

    def _rec_inputs():
        import jax
        import jax.numpy as jnp
        _rk = jax.random.key(seed)
        x = 4.136e-05 + 0.9999 * jax.random.normal(jax.random.fold_in(_rk, 1), (4, 512, 512), jnp.float32)
        _lenS = 512 - jax.random.randint(jax.random.fold_in(_rk, 7), (4,), 0, max(1, 512 // 4) + 1, jnp.int32)
        _lenS2 = 512 - jax.random.randint(jax.random.fold_in(_rk, 8), (4,), 0, max(1, 512 // 4) + 1, jnp.int32)
        _ctx_1024P = jax.random.normal(jax.random.fold_in(_rk, 11), (4, 16, 256), jnp.float32)
        _ctx_1024c = jax.random.dirichlet(jax.random.fold_in(_rk, 511), 0.3 * jnp.ones((16,), jnp.float32), (4, 512))
        _ctx_1024t = jnp.einsum('bsk,bkd->bsd', _ctx_1024c, _ctx_1024P)
        _ctx_1024t = _ctx_1024t * jax.lax.rsqrt(jnp.mean(jnp.square(_ctx_1024t)) + 1e-12) * 0.953939
        ctx_1024 = -0.000292821 + 1.00034 * (_ctx_1024t + 0.3 * jax.random.normal(jax.random.fold_in(_rk, 611), (4, 512, 256), jnp.float32))
        _g = jax.random.normal(jax.random.fold_in(_rk, 9001), (2, 1), jnp.float32)
        _g = jnp.sign(_g) * jnp.maximum(jnp.abs(_g), 1.0) + (_g == 0) * 1.0
        g_xattn = _g[0]
        g_ffn = _g[1]
        return (x, ctx_1024, g_xattn, g_ffn)
    x, ctx_1024, g_xattn, g_ffn = _rec_inputs()

    def _L0_xattn_setup():
        import jax, jax.numpy as jnp
        import numpy as np
        import math
        B, L, DM = (2, 512, 256)
        DS, DC, EXP = (16, 4, 2)
        DI = EXP * DM
        DR = math.ceil(DM / 16)
        DT_MIN, DT_MAX, DT_FLOOR = (0.001, 0.1, 0.0001)

        def _ssm_forward(hidden_states, z, in_proj_w, conv_w, conv_b, x_proj_w, dt_proj_w, dt_proj_b, A_log, D):
            b = hidden_states.shape[0]
            x = jnp.einsum('ed,bld->bel', in_proj_w, hidden_states)
            xp = jnp.pad(x, ((0, 0), (0, 0), (DC - 1, 0)))
            xc = jax.lax.conv_general_dilated(xp, conv_w[:, None, :], window_strides=(1,), padding='VALID', dimension_numbers=('NCH', 'OIH', 'NCH'), feature_group_count=DI)
            u = jax.nn.silu(xc + conv_b[None, :, None])
            x_dbl = jnp.einsum('ke,bel->bkl', x_proj_w, u)
            dt_lo = x_dbl[:, :DR]
            Bm = x_dbl[:, DR:DR + DS]
            Cm = x_dbl[:, DR + DS:]
            delta = jax.nn.softplus(jnp.einsum('er,brl->bel', dt_proj_w, dt_lo) + dt_proj_b[None, :, None])
            A = -jnp.exp(A_log)

            def step(state, xs):
                d_t, B_t, C_t, u_t = xs
                dA = jnp.exp(d_t[..., None] * A)
                state = state * dA + (d_t * u_t)[..., None] * B_t[:, None, :]
                y_t = jnp.einsum('ben,bn->be', state, C_t)
                return (state, y_t)
            xs = (jnp.moveaxis(delta, -1, 0), jnp.moveaxis(Bm, -1, 0), jnp.moveaxis(Cm, -1, 0), jnp.moveaxis(u, -1, 0))
            state0 = jnp.zeros((b, DI, DS), delta.dtype)
            _, ys = jax.lax.scan(step, state0, xs)
            y = jnp.moveaxis(ys, 0, -1)
            y = y + D[None, :, None] * u
            y = y * jax.nn.silu(z)
            return jnp.swapaxes(y, 1, 2)
        key = jax.random.key(seed)
        ks = jax.random.split(key, 8)
        hidden_states = jax.random.normal(ks[0], (B, L, DM), jnp.float32)
        z = jax.random.normal(ks[1], (B, DI, L), jnp.float32)
        in_proj_w = jax.random.normal(ks[2], (DI, DM), jnp.float32) * DM ** (-0.5)
        conv_w = jax.random.normal(ks[3], (DI, DC), jnp.float32) * DC ** (-0.5)
        conv_b = jnp.zeros((DI,), jnp.float32)
        x_proj_w = jax.random.normal(ks[4], (DR + 2 * DS, DI), jnp.float32) * DI ** (-0.5)
        dt_std = DR ** (-0.5)
        dt_proj_w = jax.random.uniform(ks[5], (DI, DR), jnp.float32, -dt_std, dt_std)
        dt = jnp.exp(jax.random.uniform(ks[6], (DI,), jnp.float32) * (math.log(DT_MAX) - math.log(DT_MIN)) + math.log(DT_MIN))
        dt = jnp.clip(dt, DT_FLOOR)
        dt_proj_b = dt + jnp.log(-jnp.expm1(-dt))
        A_log = jnp.log(jnp.broadcast_to(jnp.arange(1, DS + 1, dtype=jnp.float32), (DI, DS)))
        D = jnp.ones((DI,), jnp.float32)
        return dict(hidden_states=hidden_states, z=z, in_proj_w=in_proj_w, conv_w=conv_w, conv_b=conv_b, x_proj_w=x_proj_w, dt_proj_w=dt_proj_w, dt_proj_b=dt_proj_b, A_log=A_log, D=D)
    _L0_xattn_all = _L0_xattn_setup()
    _L0_xattn_in = {k: v for k, v in _L0_xattn_all.items() if k in ('in_proj_w', 'conv_w', 'conv_b', 'x_proj_w', 'dt_proj_w', 'dt_proj_b', 'A_log', 'D')}
    del _L0_xattn_all

    def _L0_ffn_setup():
        import jax, jax.numpy as jnp
        import numpy as np
        from jax import lax
        H = 512
        I = 352
        E = 16
        TOP_K = 6
        IS = 2 * I

        def _swiglu(x, w13_, w2_):
            gu = x @ w13_.T
            g, u = jnp.split(gu, 2, axis=-1)
            return jax.nn.silu(g) * u @ w2_.T
        key = jax.random.key(seed)
        ks = jax.random.split(key, 6)
        return {'hidden_states': jax.random.normal(ks[0], (1, 512, H), jnp.float32), 'gate_w': jax.random.normal(ks[1], (E, H), jnp.float32) * 0.02, 'w13': jax.random.normal(ks[2], (E, 2 * I, H), jnp.float32) * 0.02, 'w2': jax.random.normal(ks[3], (E, H, I), jnp.float32) * 0.02, 'sw13': jax.random.normal(ks[4], (2 * IS, H), jnp.float32) * 0.02, 'sw2': jax.random.normal(ks[5], (H, IS), jnp.float32) * 0.02}
    _L0_ffn_all = _L0_ffn_setup()
    _L0_ffn_in = {k: v for k, v in _L0_ffn_all.items() if k in ('gate_w', 'w13', 'w2', 'sw13', 'sw2')}
    del _L0_ffn_all
    return {'x': x, 'ctx_1024': ctx_1024, 'g_xattn': g_xattn, 'g_ffn': g_ffn, 'L0_xattn_in_proj_w': _L0_xattn_in['in_proj_w'], 'L0_xattn_conv_w': _L0_xattn_in['conv_w'], 'L0_xattn_conv_b': _L0_xattn_in['conv_b'], 'L0_xattn_x_proj_w': _L0_xattn_in['x_proj_w'], 'L0_xattn_dt_proj_w': _L0_xattn_in['dt_proj_w'], 'L0_xattn_dt_proj_b': _L0_xattn_in['dt_proj_b'], 'L0_xattn_A_log': _L0_xattn_in['A_log'], 'L0_xattn_D': _L0_xattn_in['D'], 'L0_ffn_gate_w': _L0_ffn_in['gate_w'], 'L0_ffn_w13': _L0_ffn_in['w13'], 'L0_ffn_w2': _L0_ffn_in['w2'], 'L0_ffn_sw13': _L0_ffn_in['sw13'], 'L0_ffn_sw2': _L0_ffn_in['sw2']}

def reference(x, ctx_1024, g_xattn, g_ffn, L0_xattn_in_proj_w, L0_xattn_conv_w, L0_xattn_conv_b, L0_xattn_x_proj_w, L0_xattn_dt_proj_w, L0_xattn_dt_proj_b, L0_xattn_A_log, L0_xattn_D, L0_ffn_gate_w, L0_ffn_w13, L0_ffn_w2, L0_ffn_sw13, L0_ffn_sw2):
    import jax
    import jax.numpy as jnp

    def _L0_xattn_ref(hidden_states, z, in_proj_w, conv_w, conv_b, x_proj_w, dt_proj_w, dt_proj_b, A_log, D):
        import jax, jax.numpy as jnp
        import numpy as np
        import math
        B, L, DM = (2, 512, 256)
        DS, DC, EXP = (16, 4, 2)
        DI = EXP * DM
        DR = math.ceil(DM / 16)
        DT_MIN, DT_MAX, DT_FLOOR = (0.001, 0.1, 0.0001)

        def _ssm_forward(hidden_states, z, in_proj_w, conv_w, conv_b, x_proj_w, dt_proj_w, dt_proj_b, A_log, D):
            b = hidden_states.shape[0]
            x = jnp.einsum('ed,bld->bel', in_proj_w, hidden_states)
            xp = jnp.pad(x, ((0, 0), (0, 0), (DC - 1, 0)))
            xc = jax.lax.conv_general_dilated(xp, conv_w[:, None, :], window_strides=(1,), padding='VALID', dimension_numbers=('NCH', 'OIH', 'NCH'), feature_group_count=DI)
            u = jax.nn.silu(xc + conv_b[None, :, None])
            x_dbl = jnp.einsum('ke,bel->bkl', x_proj_w, u)
            dt_lo = x_dbl[:, :DR]
            Bm = x_dbl[:, DR:DR + DS]
            Cm = x_dbl[:, DR + DS:]
            delta = jax.nn.softplus(jnp.einsum('er,brl->bel', dt_proj_w, dt_lo) + dt_proj_b[None, :, None])
            A = -jnp.exp(A_log)

            def step(state, xs):
                d_t, B_t, C_t, u_t = xs
                dA = jnp.exp(d_t[..., None] * A)
                state = state * dA + (d_t * u_t)[..., None] * B_t[:, None, :]
                y_t = jnp.einsum('ben,bn->be', state, C_t)
                return (state, y_t)
            xs = (jnp.moveaxis(delta, -1, 0), jnp.moveaxis(Bm, -1, 0), jnp.moveaxis(Cm, -1, 0), jnp.moveaxis(u, -1, 0))
            state0 = jnp.zeros((b, DI, DS), delta.dtype)
            _, ys = jax.lax.scan(step, state0, xs)
            y = jnp.moveaxis(ys, 0, -1)
            y = y + D[None, :, None] * u
            y = y * jax.nn.silu(z)
            return jnp.swapaxes(y, 1, 2)
        return _ssm_forward(hidden_states, z, in_proj_w, conv_w, conv_b, x_proj_w, dt_proj_w, dt_proj_b, A_log, D)

    def _L0_ffn_ref(hidden_states, gate_w, w13, w2, sw13, sw2):
        import jax, jax.numpy as jnp
        import numpy as np
        from jax import lax
        H = 512
        I = 352
        E = 16
        TOP_K = 6
        IS = 2 * I

        def _swiglu(x, w13_, w2_):
            gu = x @ w13_.T
            g, u = jnp.split(gu, 2, axis=-1)
            return jax.nn.silu(g) * u @ w2_.T
        B, S, Hd = hidden_states.shape
        x = hidden_states.reshape(-1, Hd)
        T = x.shape[0]
        scores = jax.nn.softmax(x @ gate_w.T, axis=-1)
        topk_w, topk_ids = lax.top_k(scores, TOP_K)
        topk_w = topk_w / (topk_w.sum(-1, keepdims=True) + 1e-20)
        combine = jnp.einsum('tk,tke->te', topk_w, jax.nn.one_hot(topk_ids, E, dtype=topk_w.dtype))

        def body(acc, ew):
            w13_e, w2_e, c_e = ew
            y = _swiglu(x, w13_e, w2_e)
            return (acc + c_e[:, None] * y, None)
        out, _ = lax.scan(body, jnp.zeros_like(x), (w13, w2, combine.T))
        out = out + _swiglu(x, sw13, sw2)
        return out.reshape(B, S, Hd)
    x = x + jnp.tanh(g_xattn[0]) * _L0_xattn_ref(ctx_1024, _layernorm(x, axis=-1), L0_xattn_in_proj_w, L0_xattn_conv_w, L0_xattn_conv_b, L0_xattn_x_proj_w, L0_xattn_dt_proj_w, L0_xattn_dt_proj_b, L0_xattn_A_log, L0_xattn_D)
    x = x + jnp.tanh(g_ffn[0]) * _L0_ffn_ref(_layernorm(x, axis=-1), L0_ffn_gate_w, L0_ffn_w13, L0_ffn_w2, L0_ffn_sw13, L0_ffn_sw2)
    return x

_drawn_inputs = setup_inputs


def setup_inputs(seed=0):
    import zlib

    import numpy as np

    out = dict(_drawn_inputs(seed))
    spreads = {'L0_xattn_conv_b': (0.0, 0.28), 'L0_xattn_D': (1.0, 0.2)}
    factors = {'L0_xattn_dt_proj_w': 6.688,
     'L0_xattn_dt_proj_b': 2.936,
     'L0_ffn_gate_w': 4.422,
     'L0_ffn_w13': 3.558,
     'L0_ffn_w2': 3.566}
    for name, (base, spread) in spreads.items():
        noise = np.random.default_rng([zlib.crc32(name.encode()), seed]).standard_normal(out[name].shape)
        drawn = base * np.exp(spread * noise) if base else spread * noise
        out[name] = jnp.asarray(drawn.astype(out[name].dtype))
    for name, factor in factors.items():
        out[name] = (out[name] * factor).astype(out[name].dtype)
    return out
```

```python
from contextlib import ExitStack

import concourse.bass as bass
from concourse import mybir

F32 = mybir.dt.float32
F32R = mybir.dt.float32r
I32 = mybir.dt.int32
U32 = mybir.dt.uint32
ALU = mybir.AluOpType
ACT = mybir.ActivationFunctionType
AX = mybir.AxisListType

P = 128
NB, L, H = 4, 512, 512
DM, DI, DS, DR, DC = 256, 512, 16, 16, 4
J = DI // P
TC = L // P
KC = DM // P
E, TOPK, I = 16, 6, 352
NX = E + 2
HK = H // P
IP = 384
IK = IP // P
WCOLS = HK * 2 * I + IK * H
W2AT = HK * 2 * I
ROW = H + NX + 2
TOKENS = NB * L
NT = NX * (TOKENS // P)
DTP, BP, CP, XP = 0, 32, 64, 80
LN_EPS = 1e-5

PRE_USE = {("inproj", 0): (0, 0), ("inproj", 1): (1, 0), ("inproj", 2): (0, 1), ("inproj", 3): (1, 1),
           ("xproj", 0): (0, 2), ("dt", 0): (1, 2), ("dt", 1): (0, 3), ("bt", 0): (1, 3),
           ("dt", 2): (0, 4), ("dt", 3): (1, 4),
           ("dut", 0): (0, 5), ("dut", 1): (1, 5), ("dut", 2): (0, 6), ("dut", 3): (1, 6)}
EPI_USE = {("yt", 0): (0, 0), ("yt", 1): (1, 0), ("yt", 2): (0, 1), ("yt", 3): (1, 1),
           ("xlt", 0): (0, 2), ("xlt", 1): (1, 2), ("xlt", 2): (0, 3), ("xlt", 3): (1, 3),
           ("logits", 0): (0, 4)}
PRE_N = (7, 7)
EPI_N = (5, 4)


def use(stage, i, q):
    if (stage, i) in PRE_USE:
        bank, m = PRE_USE[(stage, i)]
        return bank, q * (PRE_N[bank] + EPI_N[bank]) + m
    bank, m = EPI_USE[(stage, i)]
    if isinstance(q, int) and q == NB - 1:
        return bank, NB * PRE_N[bank] + (q + 1) * EPI_N[bank] + m
    return bank, (q + 2) * PRE_N[bank] + (q + 1) * EPI_N[bank] + m


def prelude_items(q):
    return {4: [("load", q, 0), ("stats", q, 0), ("inproj", q, 0)], 5: [("inproj", q, 1)],
            6: [("inproj", q, 2)], 7: [("inproj", q, 3)], 8: [("silu", q, 0)], 9: [("xproj", q, 0)],
            10: [("dt", q, 0), ("dt", q, 1)], 11: [("bt", q, 0), ("delta", q, 0), ("delta", q, 1)],
            12: [("dt", q, 2), ("dt", q, 3)], 13: [("delta", q, 2), ("delta", q, 3)],
            14: [("dut", q, 0), ("dut", q, 1)], 15: [("dut", q, 2), ("dut", q, 3)]}


def epilogue_items(b):
    return {0: [("y", b, 0)], 1: [("yt", b, t) for t in range(TC)], 2: [("norm", b, 0)],
            3: [("xlt", b, t) for t in range(TC)] + [("gate", b, 0)]}


def first_part():
    out = [item for n in range(4, DS) for item in prelude_items(0)[n]]
    return out + [("step", 0, n) for n in range(4)]


def batch_part(b, more):
    pre, epi = prelude_items(b + 1), epilogue_items(b)
    out = []
    for n in range(4, DS):
        out.append(("step", b, n))
        if more:
            out += pre[n]
    for n in range(4):
        if more:
            out.append(("step", b + 1, n))
        elif n == 0:
            out.append(("tail", b, 0))
        out += epi[n]
    return out


def mamba_moe(nc, x, ctxT, g_x, g_f, inT, convw, convb, xpT, dtwT, dtb, alog, dvec,
              gateT, wall, ident_d, iota_d, meta_d, out):
    rows_d = nc.dram_tensor("token_rows", (TOKENS, ROW), F32, kind="Internal").ap()
    c_d = nc.dram_tensor("c_rows", (NB, DS, L), F32, kind="Internal").ap()
    x_rows = x.rearrange("b (c p) h -> b p c h", p=P)
    out_rows = out.rearrange("b (c p) h -> b p c h", p=P)
    out_flat = out.rearrange("b s h -> (b s) h")
    rows_v = rows_d.rearrange("(b c p) h -> b p c h", p=P, c=TC)

    with ExitStack() as ctx:
        def alloc(stack, name, shape, dt=F32):
            return stack.enter_context(nc.sbuf_tensor(name, shape, dt))

        def sem(name):
            return ctx.enter_context(nc.semaphore(name))

        banks = [ctx.enter_context(nc.psum_tensor(f"bank{i}", [P, 512], F32)) for i in range(8)]
        ysum, dbu, misc = banks[0:4], banks[4:6], banks[6:8]

        ident = alloc(ctx, "ident", [P, P])
        meta = alloc(ctx, "meta", [1, 4, NT], I32)

        mem = ExitStack()
        iota16 = alloc(mem, "iota16", [P, DS])
        inw = alloc(mem, "inw", [P, KC, DI])
        xpw = alloc(mem, "xpw", [P, J, XP])
        dtw = alloc(mem, "dtw", [DR, DI])
        cw = alloc(mem, "cw", [P, J, DC])
        cb = alloc(mem, "cb", [P, J])
        dtbias = alloc(mem, "dtbias", [P, J])
        dsk = alloc(mem, "dsk", [P, J])
        aneg = alloc(mem, "aneg", [P, J, DS])
        aexp = alloc(mem, "aexp", [P, J, DS])
        gx = alloc(mem, "gx", [P, 1])
        gf = alloc(mem, "gf", [P, 1])
        tgx = alloc(mem, "tgx", [P, 1])
        tgf = alloc(mem, "tgf", [P, 1])
        gw = alloc(mem, "gw", [P, HK, E])
        eps = alloc(mem, "eps", [P, 1])
        one = alloc(mem, "one", [P, 1])
        xrow = alloc(mem, "xrow", [P, 2, TC, H])
        ctxt = alloc(mem, "ctxt", [P, KC, L])
        xpad = alloc(mem, "xpad", [P, J, L + 4])
        u = alloc(mem, "u", [P, 2, J, L])
        sz = alloc(mem, "sz", [P, 2, J, L])
        xd = alloc(mem, "xd", [XP, L])
        bst = alloc(mem, "bst", [P, TC, 6])
        bag = alloc(mem, "bag", [P, TC, 2])
        lnv = alloc(mem, "lnv", [P, TC])
        rstd = alloc(mem, "rstd", [P, TC])
        nmr = alloc(mem, "nmr", [P, TC])
        sv = alloc(mem, "sv", [P, 2, L])
        nv = alloc(mem, "nv", [P, 2, L])
        se = alloc(mem, "se", [P, 2, L])
        sw = alloc(mem, "sw", [P, 2, L])
        st1 = alloc(mem, "st1", [P, L])
        st2 = alloc(mem, "st2", [P, L])
        delta = alloc(mem, "delta", [P, 2, J, L])
        du = alloc(mem, "du", [P, J, L])
        y = du
        duT = alloc(mem, "duT", [P, 2, TC, DI])
        btn = alloc(mem, "btn", [P, TC, DS])
        btc = alloc(mem, "btc", [P, TC, DS])
        gt = alloc(mem, "gt", [P, 2, TC, DI])
        dA = alloc(mem, "dA", [P, 4, L])
        hs = alloc(mem, "hs", [P, 4, L])
        crow = alloc(mem, "crow", [P, 4, L])
        hc = alloc(mem, "hc", [P, 4, L])
        bst2 = alloc(mem, "bst2", [P, TC, 6])
        bag2 = alloc(mem, "bag2", [P, TC, 2])
        lnv2 = alloc(mem, "lnv2", [P, TC])
        rstd2 = alloc(mem, "rstd2", [P, TC])
        rowb = alloc(mem, "rowb", [P, TC, ROW])
        xlT = alloc(mem, "xlT", [P, TC, HK, P])
        mx = alloc(mem, "mx", [P, TC])
        lgs = alloc(mem, "lgs", [P, TC, E])
        ex = alloc(mem, "ex", [P, TC, E])
        sm = alloc(mem, "sm", [P, TC])
        rsm = alloc(mem, "rsm", [P, TC])
        sc = alloc(mem, "sc", [P, TC, E])
        m8 = alloc(mem, "m8", [P, TC, 8])
        ix = alloc(mem, "ix", [P, TC, 8], U32)
        ixf = alloc(mem, "ixf", [P, TC, 8])
        eq = alloc(mem, "eq", [P, TC, E, TOPK])
        mask = alloc(mem, "mask", [P, TC, E])
        s6 = alloc(mem, "s6", [P, TC])
        r6 = alloc(mem, "r6", [P, TC])
        r6g = alloc(mem, "r6g", [P, TC])
        mem.close()

        wraw = alloc(ctx, "wraw", [P, WCOLS])
        wh = alloc(ctx, "wh", [P, 2 * WCOLS], F32R)
        wl = alloc(ctx, "wl", [P, 2 * WCOLS], F32R)
        xt = alloc(ctx, "xt", [P, 2, ROW])
        xh = alloc(ctx, "xh", [P, 2, H], F32R)
        xl = alloc(ctx, "xl", [P, 2, H], F32R)
        cc = alloc(ctx, "cc", [P, 2])
        sg = alloc(ctx, "sg", [P, 2, I])
        am = alloc(ctx, "am", [P, 2, IP])
        ah = alloc(ctx, "ah", [P, 2, IP], F32R)
        al = alloc(ctx, "al", [P, 2, IP], F32R)
        ys = alloc(ctx, "ys", [P, 4, H])

        const_in = sem("const_in")
        setup_act = sem("setup_act")
        setup_dve = sem("setup_dve")
        ctx_in = sem("ctx_in")
        xrow_in = sem("xrow_in")
        full = [sem("misc_full0"), sem("misc_full1")]
        gone = [sem("misc_gone0"), sem("misc_gone1")]
        stats_done = sem("stats_done")
        lnv_done = sem("lnv_done")
        rstd_done = sem("rstd_done")
        nmr_done = sem("nmr_done")
        bst_done = sem("bst_done")
        conv_done = sem("conv_done")
        silu_done = sem("silu_done")
        cd_stored = sem("cd_stored")
        crow_in = [sem(f"crow_in{i}") for i in range(4)]
        sv_done = sem("sv_done")
        nv_done = sem("nv_done")
        se_done = sem("se_done")
        sw_done = sem("sw_done")
        st_done = sem("st_done")
        delta_done = sem("delta_done")
        du_done = sem("du_done")
        btc_done = sem("btc_done")
        g_done = sem("g_done")
        turned = sem("turned")
        dA_done = sem("dA_done")
        scanned = sem("scanned")
        hc_done = sem("hc_done")
        summed = sem("summed")
        y_done = sem("y_done")
        yz_done = sem("yz_done")
        x2_done = sem("x2_done")
        bst2_done = sem("bst2_done")
        bag2_done = sem("bag2_done")
        lnv2_done = sem("lnv2_done")
        rstd2_done = sem("rstd2_done")
        norm_done = sem("norm_done")
        base_stored = sem("base_stored")
        rows_stored = sem("rows_stored")
        gate_step = sem("gate_step")
        exp_done = sem("exp_done")
        raw_in = sem("raw_in")
        wh_done = sem("wh_done")
        wl_done = sem("wl_done")
        xt_in = [sem("xt_in0"), sem("xt_in1")]
        xt_turned = sem("xt_turned")
        xh_done = sem("xh_done")
        xl_done = sem("xl_done")
        cc_done = sem("cc_done")
        up_done = sem("up_done")
        sg_done = sem("sg_done")
        am_done = sem("am_done")
        am_turned = sem("am_turned")
        ah_done = sem("ah_done")
        al_done = sem("al_done")
        down_done = sem("down_done")
        ys_done = sem("ys_done")
        added = sem("added")
        pad_done = sem("pad_done")

        GATE_STEPS = 15
        N_CONST = 14

        def at_least(eng, s, v):
            if isinstance(v, int) and v <= 0:
                return
            eng.wait_ge(s, v)

        waited = {e: sem(f"waited_{e}") for e in ("sp", "act", "dve", "pe")}

        def apart(eng, s, v, who):
            at_least(eng, s, v)
            if not isinstance(v, int):
                eng.sem_inc(waited[who], 1)

        block = ctx.enter_context(nc.Block())

        @block.sync
        def _(sp):
            consts = [(ident, ident_d), (iota16, iota_d), (inw, inT.rearrange("(k p) e -> p k e", p=P)),
                      (xpw, xpT.rearrange("(k p) m -> p k m", p=P)), (dtw, dtwT),
                      (cw, convw.rearrange("(j p) c -> p j c", p=P)), (cb, convb.rearrange("(j p) -> p j", p=P)),
                      (dtbias, dtb.rearrange("(j p) -> p j", p=P)), (dsk, dvec.rearrange("(j p) -> p j", p=P)),
                      (aexp, alog.rearrange("(j p) n -> p j n", p=P)), (gw, gateT.rearrange("(k p) e -> p k e", p=P)),
                      (gx, g_x.partition_broadcast(P)), (gf, g_f.partition_broadcast(P)), (meta, meta_d)]
            with nc.allow_non_contiguous_dma(reason="per-channel vectors of 512 values"):
                for dst, src in consts:
                    sp.dma_start(dst[:], src).then_inc(const_in, 16)

            def load(q, _):
                if not (isinstance(q, int) and q == 0):
                    bank, m = use("inproj", 3, q - 1)
                    apart(sp, full[bank], m + 1, "sp")
                    apart(sp, nmr_done, q, "sp")
                    apart(sp, base_stored, 16 * (q - 1), "sp")
                    apart(sp, norm_done, TC * (q - 1), "sp")
                    apart(sp, silu_done, 2 * J * q, "sp")
                sp.dma_start(ctxt[:], ctxT[bass.ds(q, 1)].rearrange("a (k p) t -> p (a k) t", p=P)).then_inc(ctx_in, 16)
                sp.dma_start(xrow[:, bass.ds(q % 2, 1)].rearrange("p a c h -> p (a c) h"),
                             x_rows[bass.ds(q, 1)].rearrange("a p c h -> p (a c) h")).then_inc(xrow_in, 16)

            def xproj(q, _):
                bank, m = use("xproj", 0, q)
                apart(sp, gone[bank], m + 1, "sp")
                sp.dma_start(c_d[bass.ds(q, 1)].rearrange("a n t -> (a n) t"), xd[CP:CP + DS, :]).then_inc(cd_stored, 16)

            def step(b, n):
                if n == 0:
                    apart(sp, cd_stored, 16 * (b + 1), "sp")
                apart(sp, hc_done, (b * DS + n - 3) * J, "sp")
                src = c_d[bass.ds(b, 1), n, :].rearrange("a t -> (a t)")
                sp.dma_start(crow[:, n % 4, :], src.partition_broadcast(P)).then_inc(crow_in[n % 4], 16)

            def norm(b, _):
                apart(sp, x2_done, TC * (b + 1), "sp")
                sp.dma_start(out_rows[bass.ds(b, 1)].rearrange("a p c h -> p (a c) h"), xrow[:, bass.ds(b % 2, 1)].rearrange("p a c h -> p (a c) h")).then_inc(base_stored, 16)

            def gate(b, _):
                apart(sp, gate_step, GATE_STEPS * (b + 1), "sp")
                apart(sp, norm_done, TC * (b + 1), "sp")
                sp.dma_start(rows_v[bass.ds(b, 1)].rearrange("a p c h -> p (a c) h"), rowb[:]).then_inc(rows_stored, 16)

            work = {"load": load, "xproj": xproj, "step": step, "norm": norm, "gate": gate}

            def run(items):
                for kind, b, i in items:
                    if kind in work:
                        work[kind](b, i)

            run(first_part())
            with sp.Fori(0, NB - 1) as b:
                run(batch_part(b, True))
            run(batch_part(NB - 1, False))

            sp.wait_ge(rows_stored, 16 * NB)
            sp.wait_ge(norm_done, TC * NB)

            def tile_in(t, s, r):
                at_least(sp, xt_turned, t - 1)
                at_least(sp, cc_done, t - 1)
                sp.dma_start(xt[:, s, :], rows_d[bass.ds(r, P), :]).then_inc(xt_in[s], 16)

            with sp.Fori(0, NT // 2) as i:
                for s in range(2):
                    r = sp.value_load(meta[0:1, 0, bass.ds(2 * i + s, 1)], min_val=0, max_val=TOKENS - P)
                    if s == 0:
                        sp.wait_ge(xt_turned, 2 * i)
                        sp.wait_ge(cc_done, 2 * i)
                    tile_in(2 * i + s, s, r) if s else \
                        sp.dma_start(xt[:, 0, :], rows_d[bass.ds(r, P), :]).then_inc(xt_in[0], 16)

            sp.wait_ge(base_stored, 16 * NB)
            sp.wait_ge(added, 16 * NT)

        @block.scalar
        def _(act):
            act.wait_ge(const_in, 16 * N_CONST)
            nc.scalar.activation(aneg[:], aexp[:], ACT.Exp).then_inc(setup_act, 1)
            nc.scalar.activation(tgx[:], gx[:], ACT.Tanh).then_inc(setup_act, 1)
            nc.scalar.activation(tgf[:], gf[:], ACT.Tanh).then_inc(setup_act, 1)
            act.wait_ge(setup_dve, 1)

            def evacuate(stage, i, q, dst, cols, parts=P):
                bank, m = use(stage, i, q)
                apart(act, full[bank], m + 1, "act")
                nc.scalar.copy(dst, misc[bank][0:parts, 0:cols]).then_inc(gone[bank], 1)

            def stats(q, _):
                act.wait_ge(stats_done, q + 1)
                at_least(act, nmr_done, q)
                nc.scalar.activation(lnv[:], bag[:, :, 1], ACT.Ln, bias=eps[:]).then_inc(lnv_done, 1)
                act.wait_ge(lnv_done, q + 1)
                at_least(act, silu_done, 2 * J * q)
                nc.scalar.activation(rstd[:], lnv[:], ACT.Exp, scale=-0.5).then_inc(rstd_done, 1)

            def inproj(q, j):
                at_least(act, conv_done, DC * (J * (q - 1) + j + 1) if not (isinstance(q, int) and q == 0) else 0)
                evacuate("inproj", j, q, xpad[:, j, 3:3 + L], L)

            def silu(q, _):
                for j in range(J):
                    apart(act, conv_done, DC * (J * q + j + 1), "act")
                    uj = u[:, bass.ds(q % 2, 1), j, :].rearrange("p a t -> p (a t)")
                    nc.scalar.activation(uj, uj, ACT.Silu, bias=cb[:, j:j + 1]).then_inc(silu_done, 1)
                apart(act, nmr_done, q + 1, "act")
                apart(act, yz_done, J * (q - 1), "act")
                for j in range(J):
                    nc.scalar.activation(sz[:, bass.ds(q % 2, 1), j, :].rearrange("p a t -> p (a t)"),
                                         xrow[:, bass.ds(q % 2, 1), j, :].rearrange("p a t -> p (a t)"),
                                         ACT.Silu, bias=nmr[:, j:j + 1], scale=rstd[:, j:j + 1]).then_inc(silu_done, 1)

            def xproj(q, _):
                at_least(act, cd_stored, 16 * q)
                if not (isinstance(q, int) and q == 0):
                    bank, m = use("dt", 3, q - 1)
                    act.wait_ge(full[bank], m + 1)
                evacuate("xproj", 0, q, xd[:], L, XP)

            def bt(q, _):
                evacuate("bt", 0, q, btn[:].rearrange("p c n -> p (c n)"), TC * DS)

            def dt(q, j):
                act.wait_ge(nv_done, J * q + j + 1)
                at_least(act, st_done, 3 * (J * q + j - 1))
                nc.scalar.activation(se[:, j % 2, :], nv[:, j % 2, :], ACT.Exp).then_inc(se_done, 1)
                act.wait_ge(se_done, J * q + j + 1)
                nc.scalar.activation(sw[:, j % 2, :], se[:, j % 2, :], ACT.Ln, bias=one[:]).then_inc(sw_done, 1)

            def dut(q, t):
                evacuate("dut", t, q, duT[:, bass.ds(q % 2, 1), t, :].rearrange("p a t -> p (a t)"), DI)

            def step(b, n):
                if n == 0:
                    bank, m = use("dut", 3, b)
                    act.wait_ge(gone[bank], m + 1)
                    at_least(act, g_done, DS * b)
                    nc.scalar.copy(btc[:], btn[:]).then_inc(btc_done, 1)
                    apart(act, btc_done, b + 1, "act")
                    bank, m = use("dut", 2, b)
                    apart(act, gone[bank], m + 1, "act")
                    apart(act, delta_done, J * (b + 1), "act")
                apart(act, turned, J * (b * DS + n - 1), "act")
                for t in range(TC):
                    g = nc.scalar.activation(gt[:, n % 2, t, :], duT[:, bass.ds(b % 2, 1), t, :].rearrange("p a t -> p (a t)"),
                                             ACT.Copy, scale=btc[:, t, n:n + 1])
                g.then_inc(g_done, 1)
                for j in range(J):
                    apart(act, scanned, (b * DS + n - 1) * J + j + 1, "act")
                    nc.scalar.activation(dA[:, j, :], delta[:, bass.ds(b % 2, 1), j, :].rearrange("p a t -> p (a t)"),
                                         ACT.Exp, scale=aneg[:, j, n:n + 1]).then_inc(dA_done, 1)

            def norm(b, _):
                act.wait_ge(bag2_done, b + 1)
                at_least(act, norm_done, TC * b)
                nc.scalar.activation(lnv2[:], bag2[:, :, 1], ACT.Ln, bias=eps[:]).then_inc(lnv2_done, 1)
                act.wait_ge(lnv2_done, b + 1)
                nc.scalar.activation(rstd2[:], lnv2[:], ACT.Exp, scale=-0.5).then_inc(rstd2_done, 1)

            def xlt(b, t):
                evacuate("xlt", t, b, xlT[:, t, :, :].rearrange("p k m -> p (k m)"), H)

            def gate(b, _):
                bank, m = use("logits", 0, b)
                act.wait_ge(gone[bank], m + 1)
                nc.scalar.activation(ex[:], lgs[:], ACT.Exp).then_inc(exp_done, 1)

            work = {"stats": stats, "inproj": inproj, "silu": silu, "xproj": xproj, "bt": bt, "dt": dt,
                    "dut": dut, "step": step, "norm": norm, "xlt": xlt, "gate": gate}

            def run(items):
                for kind, b, i in items:
                    if kind in work:
                        work[kind](b, i)

            act.wait_ge(setup_dve, 2)
            run(first_part())
            with act.Fori(0, NB - 1) as b:
                run(batch_part(b, True))
            run(batch_part(NB - 1, False))

            def x_high(t, s):
                act.wait_ge(xt_turned, t + 1)
                at_least(act, up_done, t - 1)
                nc.scalar.copy(xh[:, s, :], banks[0][:]).then_inc(xh_done, 1)

            def gate_up(t, s):
                act.wait_ge(up_done, t + 1)
                at_least(act, am_done, t - 1)
                nc.scalar.activation(sg[:, s, :], banks[1 + 2 * s][:, 0:I], ACT.Silu).then_inc(sg_done, 1)

            def a_high(t, s):
                act.wait_ge(am_turned, t + 1)
                at_least(act, down_done, t - 1)
                nc.scalar.copy(ah[:, s, :], banks[5][:, 0:IP]).then_inc(ah_done, 1)

            def y_out(t, s, slot):
                apart(act, down_done, t + 1, "act")
                apart(act, added, 16 * (t - 3), "act")
                nc.scalar.copy(ys[:, bass.ds(slot, 1), :].rearrange("p a h -> p (a h)"), banks[6 + s][:]).then_inc(ys_done, 1)

            x_high(0, 0)
            x_high(1, 1)
            gate_up(0, 0)
            for t in (1, 2, 3, 4):
                a_high(t - 1, (t - 1) % 2)
                x_high(t + 1, (t + 1) % 2)
                gate_up(t, t % 2)
                y_out(t - 1, (t - 1) % 2, t - 1)
            with act.Fori(2, NT // 2 - 1) as i:
                for k in (1, 2):
                    t, s = 2 * i + k, k % 2
                    a_high(t - 1, 1 - s)
                    x_high(t + 1, 1 - s)
                    gate_up(t, s)
                    y_out(t - 1, 1 - s, (t - 1) % 4)
            a_high(NT - 2, 0)
            gate_up(NT - 1, 1)
            y_out(NT - 2, 0, (NT - 2) % 4)
            a_high(NT - 1, 1)
            y_out(NT - 1, 1, (NT - 1) % 4)

        @block.gpsimd
        def _(pool):
            def step(b, n):
                pool.wait_ge(crow_in[n % 4], 16 * (b * (DS // 4) + n // 4 + 1))
                for j in range(J):
                    i = (b * DS + n) * J + j
                    pool.wait_ge(scanned, i + 1)
                    at_least(pool, summed, i - 3)
                    nc.gpsimd.tensor_tensor(hc[:, j, :], hs[:, j, :], crow[:, n % 4, :], ALU.mult).then_inc(hc_done, 1)

            def run(items):
                for kind, b, n in items:
                    if kind == "step":
                        step(b, n)

            run(first_part())
            with pool.Fori(0, NB - 1) as b:
                run(batch_part(b, True))
            run(batch_part(NB - 1, False))

            pool.wait_ge(rows_stored, 16 * NB)
            pool.wait_ge(base_stored, 16 * NB)

            def fetch(e):
                pool.dma_start(wraw[:], wall[bass.ds(e, 1)].rearrange("a p c -> p (a c)")).then_inc(raw_in, 16)

            def split(e):
                half = bass.ds((e % 2) * WCOLS, WCOLS)
                pool.wait_ge(raw_in, 16 * (e + 1))
                if not isinstance(e, int) or e > 1:
                    pool.wait_ge(down_done, (e - 1) * (TOKENS // P))
                nc.gpsimd.tensor_copy(wh[:, half], wraw[:]).then_inc(wh_done, 1)
                pool.wait_ge(wh_done, e + 1)
                nc.gpsimd.tensor_tensor(wl[:, half], wraw[:], wh[:, half], ALU.subtract).then_inc(wl_done, 1)

            def add_tiles(e):
                with pool.Fori(0, TOKENS // P) as i:
                    t = pool.snap(e * (TOKENS // P) + i)
                    r = pool.value_load(meta[0:1, 0, bass.ds(t, 1)], min_val=0, max_val=TOKENS - P)
                    pool.wait_ge(ys_done, t + 1)
                    pool.wait_ge(added, 16 * t)
                    pool.dma_start(out_flat[bass.ds(r, P), :], ys[:, bass.ds(t % 4, 1), :].rearrange("p a h -> p (a h)"),
                                   accum_op=ALU.add).then_inc(added, 16)

            fetch(0)
            split(0)
            pool.wait_ge(wl_done, 1)
            fetch(1)
            split(1)
            pool.wait_ge(wl_done, 2)
            fetch(2)
            add_tiles(0)
            with pool.Fori(1, NX - 2) as e:
                split(e + 1)
                pool.wait_ge(wl_done, e + 2)
                fetch(e + 2)
                add_tiles(e)
            split(NX - 1)
            add_tiles(NX - 2)
            add_tiles(NX - 1)

        @block.vector
        def _(dve):
            nc.vector.memset(eps[:], LN_EPS)
            nc.vector.memset(one[:], 1.0)
            nc.vector.memset(xpad[:], 0.0).then_inc(setup_dve, 1)
            dve.wait_ge(setup_act, 3)
            nc.vector.tensor_scalar(aneg[:], aneg[:], -1.0, None, ALU.mult).then_inc(setup_dve, 1)
            nc.vector.memset(rowb[:], 1.0).then_inc(setup_dve, 1)
            dve.wait_ge(setup_dve, 3)
            nc.vector.tensor_scalar(rowb[:, :, H + E:ROW], rowb[:, :, H + E:ROW], tgf[:, 0:1], None,
                                    ALU.mult).then_inc(setup_dve, 1)

            def stats(q, _):
                apart(dve, xrow_in, 16 * (q + 1), "dve")
                apart(dve, stats_done, q, "dve")
                for c in range(TC):
                    nc.vector.bn_stats(bst[:, c, :], xrow[:, bass.ds(q % 2, 1), c, :].rearrange("p a h -> p (a h)")).then_inc(bst_done, 1)
                apart(dve, bst_done, TC * (q + 1), "dve")
                apart(dve, nmr_done, q, "dve")
                for c in range(TC):
                    ins = nc.vector.bn_aggr(bag[:, c, :], bst[:, c, :])
                ins.then_inc(stats_done, 1)
                dve.wait_ge(rstd_done, q + 1)
                dve.wait_ge(stats_done, q + 1)
                at_least(dve, silu_done, 2 * J * q)
                nc.vector.scalar_tensor_tensor(out=nmr[:], in0=bag[:, :, 0], scalar=-1.0, in1=rstd[:],
                                               op0=ALU.mult, op1=ALU.mult).then_inc(nmr_done, 1)

            def inproj(q, j):
                bank, m = use("inproj", j, q)
                dve.wait_ge(gone[bank], m + 1)
                if j == 0:
                    at_least(dve, y_done, J * (q - 1))
                uj = u[:, bass.ds(q % 2, 1), j, :].rearrange("p a t -> p (a t)")
                nc.vector.tensor_scalar(uj, xpad[:, j, 3:3 + L], cw[:, j, 3:4], None, ALU.mult).then_inc(conv_done, 1)
                for k in (2, 1, 0):
                    dve.wait_ge(conv_done, DC * (J * q + j) + 3 - k)
                    nc.vector.scalar_tensor_tensor(out=uj, in0=xpad[:, j, k:k + L], scalar=cw[:, j, k:k + 1], in1=uj,
                                                   op0=ALU.mult, op1=ALU.add).then_inc(conv_done, 1)

            def dt(q, j):
                bank, m = use("dt", j, q)
                dve.wait_ge(full[bank], m + 1)
                at_least(dve, delta_done, J * q + j - 1)
                nc.vector.tensor_scalar(sv[:, j % 2, :], misc[bank][:], dtbias[:, j:j + 1], None, ALU.add).then_inc(gone[bank], 1)
                dve.wait_ge(gone[bank], m + 1)
                nc.vector.scalar_tensor_tensor(out=nv[:, j % 2, :], in0=sv[:, j % 2, :], scalar=-1.0, in1=sv[:, j % 2, :],
                                               op0=ALU.mult, op1=ALU.min).then_inc(nv_done, 1)

            def delta_(q, j):
                i = J * q + j
                dve.wait_ge(sw_done, i + 1)
                at_least(dve, st_done, 3 * i)
                nc.vector.tensor_scalar(st1[:], se[:, j % 2, :], 1.0, -1.0, ALU.add, ALU.add).then_inc(st_done, 1)
                dve.wait_ge(st_done, 3 * i + 1)
                nc.vector.tensor_tensor(st2[:], se[:, j % 2, :], st1[:], ALU.subtract).then_inc(st_done, 1)
                dve.wait_ge(st_done, 3 * i + 2)
                nc.vector.tensor_tensor(st1[:], sw[:, j % 2, :], st2[:], ALU.add).then_inc(st_done, 1)
                dve.wait_ge(st_done, 3 * i + 3)
                if j == 0:
                    at_least(dve, dA_done, (q - 1) * DS * J)
                dj = delta[:, bass.ds(q % 2, 1), j, :].rearrange("p a t -> p (a t)")
                nc.vector.scalar_tensor_tensor(out=dj, in0=sv[:, j % 2, :], scalar=0.0, in1=st1[:],
                                               op0=ALU.max, op1=ALU.add).then_inc(delta_done, 1)
                dve.wait_ge(delta_done, i + 1)
                dve.wait_ge(silu_done, 2 * J * q + j + 1)
                if not (isinstance(q, int) and q == 0):
                    bank, m = use("yt", 3, q - 2)
                    dve.wait_ge(full[bank], m + 1)
                nc.vector.tensor_tensor(du[:, j, :], dj, u[:, bass.ds(q % 2, 1), j, :].rearrange("p a t -> p (a t)"),
                                        ALU.mult).then_inc(du_done, 1)

            def step(b, n):
                for j in range(J):
                    i = (b * DS + n) * J + j
                    dve.wait_ge(dA_done, i + 1)
                    dve.wait_ge(turned, i + 1)
                    at_least(dve, hc_done, i - 3)
                    nc.vector.tensor_tensor_scan(hs[:, j, :], dA[:, j, :], dbu[j % 2][:], 0.0,
                                                 ALU.mult, ALU.add).then_inc(scanned, 1)

            def y_(b, _):
                bank, m = use("dut", 3, b if isinstance(b, int) and b == NB - 1 else b + 1)
                dve.wait_ge(full[bank], m + 1)
                for j in range(J):
                    dve.wait_ge(summed, ((b + 1) * DS - 1) * J + j + 1)
                    nc.vector.scalar_tensor_tensor(out=y[:, j, :], in0=u[:, bass.ds(b % 2, 1), j, :].rearrange("p a t -> p (a t)"),
                                                   scalar=dsk[:, j:j + 1], in1=ysum[j][:],
                                                   op0=ALU.mult, op1=ALU.add).then_inc(y_done, 1)
                for j in range(J):
                    dve.wait_ge(y_done, J * b + j + 1)
                    nc.vector.tensor_tensor(y[:, j, :], y[:, j, :], sz[:, bass.ds(b % 2, 1), j, :].rearrange("p a t -> p (a t)"),
                                            ALU.mult).then_inc(yz_done, 1)

            def yt(b, t):
                bank, m = use("yt", t, b)
                dve.wait_ge(full[bank], m + 1)
                if t == 0:
                    dve.wait_ge(silu_done, 2 * J * (b + 1))
                x2 = xrow[:, bass.ds(b % 2, 1), t, :].rearrange("p a h -> p (a h)")
                nc.vector.scalar_tensor_tensor(out=x2, in0=misc[bank][:], scalar=tgx[:, 0:1],
                                               in1=x2,
                                               op0=ALU.mult, op1=ALU.add).then_inc(gone[bank], 1)
                apart(dve, gone[bank], m + 1, "dve")
                apart(dve, bag2_done, b, "dve")
                nc.vector.bn_stats(bst2[:, t, :], x2).then_inc(x2_done, 1)

            def norm(b, _):
                apart(dve, x2_done, TC * (b + 1), "dve")
                for t in range(TC):
                    ins = nc.vector.bn_aggr(bag2[:, t, :], bst2[:, t, :])
                ins.then_inc(bag2_done, 1)
                dve.wait_ge(bag2_done, b + 1)
                dve.wait_ge(rstd2_done, b + 1)
                at_least(dve, rows_stored, 16 * b)
                for t in range(TC):
                    x2 = xrow[:, bass.ds(b % 2, 1), t, :].rearrange("p a h -> p (a h)")
                    nc.vector.tensor_scalar(rowb[:, t, 0:H], x2, bag2[:, t, 0:1], rstd2[:, t:t + 1],
                                            ALU.subtract, ALU.mult).then_inc(norm_done, 1)

            def gate(b, _):
                done = [0]
                steps = GATE_STEPS * b

                def chained(ins):
                    ins.then_inc(gate_step, 1)
                    done[0] += 1
                    apart(dve, gate_step, steps + done[0], "dve")

                bank, m = use("logits", 0, b)
                logits = misc[bank][:, 0:TC * E].rearrange("p (c e) -> p c e", e=E)
                dve.wait_ge(full[bank], m + 1)
                chained(nc.vector.tensor_reduce(mx[:], logits, AX.X, ALU.max))
                nc.vector.tensor_tensor(lgs[:], logits, mx[:].unsqueeze(2).to_broadcast([P, TC, E]),
                                        ALU.subtract).then_inc(gone[bank], 1)
                dve.wait_ge(exp_done, b + 1)
                chained(nc.vector.tensor_reduce(sm[:], ex[:], AX.X, ALU.add))
                chained(nc.vector.reciprocal(rsm[:], sm[:]))
                chained(nc.vector.tensor_tensor(sc[:], ex[:], rsm[:].unsqueeze(2).to_broadcast([P, TC, E]), ALU.mult))
                for t in range(TC):
                    ins = nc.vector.max(m8[:, t, :], sc[:, t, :])
                chained(ins)
                for t in range(TC):
                    ins = nc.vector.max_index(ix[:, t, :], m8[:, t, :], sc[:, t, :])
                chained(ins)
                chained(nc.vector.tensor_copy(ixf[:], ix[:]))
                chained(nc.vector.tensor_tensor(
                    eq[:], iota16[:].unsqueeze(1).unsqueeze(3).to_broadcast([P, TC, E, TOPK]),
                    ixf[:, :, 0:TOPK].unsqueeze(2).to_broadcast([P, TC, E, TOPK]), ALU.is_equal))
                chained(nc.vector.tensor_reduce(mask[:], eq[:], AX.X, ALU.add))
                chained(nc.vector.tensor_tensor(mask[:], mask[:], sc[:], ALU.mult))
                chained(nc.vector.tensor_reduce(s6[:], m8[:, :, 0:TOPK], AX.X, ALU.add))
                chained(nc.vector.tensor_scalar(s6[:], s6[:], 1e-20, None, ALU.add))
                chained(nc.vector.reciprocal(r6[:], s6[:]))
                chained(nc.vector.tensor_scalar(r6g[:], r6[:], tgf[:, 0:1], None, ALU.mult))
                chained(nc.vector.tensor_tensor(rowb[:, :, H:H + E], mask[:], r6g[:].unsqueeze(2).to_broadcast([P, TC, E]), ALU.mult))
                assert done[0] == GATE_STEPS

            work = {"stats": stats, "inproj": inproj, "dt": dt, "delta": delta_, "step": step, "y": y_, "yt": yt,
                    "norm": norm, "gate": gate}

            def run(items):
                for kind, b, i in items:
                    if kind in work:
                        work[kind](b, i)

            run(first_part())
            with dve.Fori(0, NB - 1) as b:
                run(batch_part(b, True))
            run(batch_part(NB - 1, False))

            dve.wait_ge(rows_stored, 16 * NB)
            dve.wait_ge(base_stored, 16 * NB)
            nc.vector.memset(am[:], 0.0).then_inc(pad_done, 1)
            dve.wait_ge(pad_done, 1)

            def x_low(t, s):
                dve.wait_ge(xh_done, t + 1)
                at_least(dve, up_done, t - 1)
                nc.vector.tensor_tensor(xl[:, s, :], banks[0][:], xh[:, s, :], ALU.subtract).then_inc(xl_done, 1)

            def take_weight(t, s, slots):
                e = dve.value_load(meta[0:1, 1, bass.ds(t, 1)], min_val=0, max_val=NX - 1)
                dve.wait_ge(xt_in[s], slots)
                at_least(dve, am_done, t - 1)
                nc.vector.tensor_copy(cc[:, s:s + 1], xt[:, s, bass.ds(H + e, 1)]).then_inc(cc_done, 1)

            def multiply(t, s):
                dve.wait_ge(sg_done, t + 1)
                dve.wait_ge(cc_done, t + 1)
                at_least(dve, am_turned, t - 1)
                nc.vector.scalar_tensor_tensor(out=am[:, s, 0:I], in0=sg[:, s, :], scalar=cc[:, s:s + 1],
                                               in1=banks[2 + 2 * s][:, 0:I], op0=ALU.mult, op1=ALU.mult).then_inc(am_done, 1)

            def a_low(t, s):
                dve.wait_ge(ah_done, t + 1)
                at_least(dve, down_done, t - 1)
                nc.vector.tensor_tensor(al[:, s, :], banks[5][:, 0:IP], ah[:, s, :], ALU.subtract).then_inc(al_done, 1)

            take_weight(0, 0, 16)
            x_low(0, 0)
            take_weight(1, 1, 16)
            x_low(1, 1)
            multiply(0, 0)
            for t in (1, 2):
                a_low(t - 1, (t - 1) % 2)
                take_weight(t + 1, (t + 1) % 2, 16 * ((t + 1) // 2 + 1))
                x_low(t + 1, (t + 1) % 2)
                multiply(t, t % 2)
            with dve.Fori(1, NT // 2 - 1) as i:
                for k in (1, 2):
                    t, s = 2 * i + k, k % 2
                    a_low(t - 1, 1 - s)
                    take_weight(t + 1, 1 - s, 16 * (i + 1 + 1))
                    x_low(t + 1, 1 - s)
                    multiply(t, s)
            a_low(NT - 2, 0)
            multiply(NT - 1, 1)
            a_low(NT - 1, 1)

        @block.tensor
        def _(pe):
            pe.wait_ge(const_in, 16 * N_CONST)

            def claim(stage, i, q, held=False):
                bank, m = use(stage, i, q)
                if held:
                    apart(pe, gone[bank], m, "pe")
                else:
                    at_least(pe, gone[bank], m)
                return misc[bank], full[bank]

            def inproj(q, j):
                pe.wait_ge(ctx_in, 16 * (q + 1))
                bank, done = claim("inproj", j, q)
                for k in range(KC):
                    mm = nc.tensor.matmul(bank[:], inw[:, k, j * P:(j + 1) * P], ctxt[:, k, :], start=k == 0, stop=k == KC - 1)
                mm.then_inc(done, 1)

            def xproj(q, _):
                pe.wait_ge(silu_done, 2 * J * q + J)
                bank, done = claim("xproj", 0, q)
                for k in range(J):
                    mm = nc.tensor.matmul(bank[0:XP, :], xpw[:, k, :], u[:, bass.ds(q % 2, 1), k, :].rearrange("p a t -> p (a t)"),
                                          start=k == 0, stop=k == J - 1)
                mm.then_inc(done, 1)

            def dt(q, j):
                if j == 0:
                    xb, xm = use("xproj", 0, q)
                    pe.wait_ge(gone[xb], xm + 1)
                bank, done = claim("dt", j, q)
                nc.tensor.matmul(bank[:], dtw[:, j * P:(j + 1) * P], xd[DTP:DTP + DR, :], start=True, stop=True).then_inc(done, 1)

            def bt(q, _):
                bank, done = claim("bt", 0, q, True)
                if not (isinstance(q, int) and q == 0):
                    apart(pe, btc_done, q, "pe")
                for t in range(TC):
                    mm = nc.tensor.transpose(bank[:, t * DS:(t + 1) * DS], xd[BP:BP + DS, t * P:(t + 1) * P], ident[BP:BP + DS, BP:BP + DS])
                mm.then_inc(done, 1)

            def dut(q, t):
                pe.wait_ge(du_done, J * (q + 1))
                bank, done = claim("dut", t, q)
                for j in range(J):
                    mm = nc.tensor.transpose(bank[:, j * P:(j + 1) * P], du[:, j, t * P:(t + 1) * P], ident[:])
                mm.then_inc(done, 1)

            def add_products(b, n):
                for j in range(J):
                    pe.wait_ge(hc_done, (b * DS + n) * J + j + 1)
                    if n == 0:
                        at_least(pe, y_done, J * (b - 1) + j + 1)
                    nc.tensor.matmul(ysum[j][:], ident[:], hc[:, j, :], start=n == 0, stop=n == DS - 1,
                                     skip_group_check=True).then_inc(summed, 1)

            def step(b, n):
                pe.wait_ge(g_done, b * DS + n + 1)
                for j in range(J):
                    at_least(pe, scanned, (b * DS + n) * J + j - 1)
                    for t in range(TC):
                        mm = nc.tensor.transpose(dbu[j % 2][:, t * P:(t + 1) * P], gt[:, n % 2, t, j * P:(j + 1) * P], ident[:])
                    mm.then_inc(turned, 1)
                if n > 0:
                    add_products(b, n - 1)
                elif not (isinstance(b, int) and b == 0):
                    add_products(b - 1, DS - 1)

            def tail(b, _):
                add_products(b, DS - 1)

            def yt(b, t):
                pe.wait_ge(yz_done, J * (b + 1))
                bank, done = claim("yt", t, b)
                for j in range(J):
                    mm = nc.tensor.transpose(bank[:, j * P:(j + 1) * P], y[:, j, t * P:(t + 1) * P], ident[:])
                mm.then_inc(done, 1)

            def xlt(b, t):
                pe.wait_ge(norm_done, TC * b + t + 1)
                bank, done = claim("xlt", t, b)
                for k in range(HK):
                    mm = nc.tensor.transpose(bank[:, k * P:(k + 1) * P], rowb[:, t, k * P:(k + 1) * P], ident[:])
                mm.then_inc(done, 1)

            def gate(b, _):
                xb, xm = use("xlt", 3, b)
                pe.wait_ge(gone[xb], xm + 1)
                bank, done = claim("logits", 0, b)
                for t in range(TC):
                    for k in range(HK):
                        mm = nc.tensor.matmul(bank[:, t * E:(t + 1) * E], xlT[:, t, k, :], gw[:, k, :],
                                              start=k == 0, stop=k == HK - 1)
                mm.then_inc(done, 1)

            work = {"inproj": inproj, "xproj": xproj, "bt": bt, "dt": dt, "dut": dut, "step": step, "tail": tail,
                    "yt": yt, "xlt": xlt, "gate": gate}

            def run(items):
                for kind, b, i in items:
                    if kind in work:
                        work[kind](b, i)

            run(first_part())
            for k in range(2):
                pe.wait_ge(gone[k], PRE_N[k])
                pe.sem_inc(full[k], EPI_N[k])
                pe.sem_inc(gone[k], EPI_N[k])
            with pe.Fori(0, NB - 1) as b:
                run(batch_part(b, True))
            run(batch_part(NB - 1, False))

            pe.wait_ge(rows_stored, 16 * NB)

            def turn_x(t, s, slots):
                pe.wait_ge(xt_in[s], slots)
                at_least(pe, xl_done, t)
                for k in range(HK):
                    mm = nc.tensor.transpose(banks[0][:, k * P:(k + 1) * P], xt[:, s, k * P:(k + 1) * P], ident[:])
                mm.then_inc(xt_turned, 1)

            def up(t, s, chunks, off):
                gate_bank, up_bank = banks[1 + 2 * s], banks[2 + 2 * s]
                if chunks[0] == 0:
                    pe.wait_ge(xl_done, t + 1)
                    at_least(pe, am_done, t - 1)
                for k in chunks:
                    high, low = xh[:, s, k * P:(k + 1) * P], xl[:, s, k * P:(k + 1) * P]
                    for n, (xx, ww) in enumerate(((high, wh), (high, wl), (low, wh))):
                        first, last = k == 0 and n == 0, k == HK - 1 and n == 2
                        nc.tensor.matmul(gate_bank[:, 0:I], xx, ww[:, bass.ds(off + k * 2 * I, I)], start=first, stop=last)
                        mm = nc.tensor.matmul(up_bank[:, 0:I], xx, ww[:, bass.ds(off + k * 2 * I + I, I)], start=first, stop=last)
                if chunks[-1] == HK - 1:
                    mm.then_inc(up_done, 1)

            def turn_a(t, s):
                pe.wait_ge(am_done, t + 1)
                at_least(pe, al_done, t)
                for k in range(IK):
                    mm = nc.tensor.transpose(banks[5][:, k * P:(k + 1) * P], am[:, s, k * P:(k + 1) * P], ident[:])
                mm.then_inc(am_turned, 1)

            def down(t, s, off):
                pe.wait_ge(al_done, t + 1)
                at_least(pe, ys_done, t - 1)
                for k in range(IK):
                    high, low = ah[:, s, k * P:(k + 1) * P], al[:, s, k * P:(k + 1) * P]
                    for n, (aa, ww) in enumerate(((high, wh), (high, wl), (low, wh))):
                        mm = nc.tensor.matmul(banks[6 + s][:], aa, ww[:, bass.ds(off + W2AT + k * H, H)],
                                              start=k == 0 and n == 0, stop=k == IK - 1 and n == 2)
                mm.then_inc(down_done, 1)

            def weights_of(t):
                e = pe.value_load(meta[0:1, 1, bass.ds(t, 1)], min_val=0, max_val=NX - 1)
                apart(pe, wl_done, e + 1, "pe")
                return pe.value_load(meta[0:1, 2, bass.ds(t, 1)], min_val=0, max_val=WCOLS)

            def tile(t, s, slots, off):
                old = pe.value_load(meta[0:1, 2, bass.ds(t - 1, 1)], min_val=0, max_val=WCOLS)
                up(t, s, (0, 1), off)
                turn_a(t - 1, 1 - s)
                up(t, s, (2, 3), off)
                if slots is not None:
                    turn_x(t + 1, 1 - s, slots)
                down(t - 1, 1 - s, old)

            turn_x(0, 0, 16)
            turn_x(1, 1, 16)
            off = weights_of(0)
            up(0, 0, (0, 1, 2, 3), off)
            for t in (1, 2):
                tile(t, t % 2, 16 * ((t + 1) // 2 + 1), weights_of(t))
            with pe.Fori(1, NT // 2 - 1) as i:
                for k in (1, 2):
                    tile(2 * i + k, k % 2, 16 * (i + 2), weights_of(2 * i + k))
            tile(NT - 1, 1, None, weights_of(NT - 1))
            turn_a(NT - 1, 1)
            down(NT - 1, 1, pe.value_load(meta[0:1, 2, NT - 1:NT], min_val=0, max_val=WCOLS))


def kernel(**inputs):
    import numpy as np
    import concourse.bacc as bacc
    from concourse.bass_utils import run_bass_kernel_spmd

    a = {k: np.asarray(v) for k, v in inputs.items()}
    f = a["x"].dtype
    xp = a["L0_xattn_x_proj_w"]
    xpT = np.zeros((DI, XP), f)
    xpT[:, DTP:DTP + DR] = xp[:DR].T
    xpT[:, BP:BP + DS] = xp[DR:DR + DS].T
    xpT[:, CP:CP + DS] = xp[DR + DS:].T
    s13, s2 = a["L0_ffn_sw13"], a["L0_ffn_sw2"]
    w13 = np.concatenate([a["L0_ffn_w13"], np.stack([np.concatenate([s13[I * i:I * i + I], s13[2 * I + I * i:3 * I + I * i]]) for i in range(2)])])
    w2 = np.concatenate([a["L0_ffn_w2"], np.stack([s2[:, I * i:I * i + I] for i in range(2)])])
    wall = np.zeros((NX, P, WCOLS), f)
    wall[:, :, :W2AT] = w13.transpose(0, 2, 1).reshape(NX, HK, P, 2 * I).transpose(0, 2, 1, 3).reshape(NX, P, W2AT)
    w2p = np.zeros((NX, IP, H), f)
    w2p[:, :I] = w2.transpose(0, 2, 1)
    wall[:, :, W2AT:] = w2p.reshape(NX, IK, P, H).transpose(0, 2, 1, 3).reshape(NX, P, IK * H)
    tiles = np.arange(NT)
    meta = np.zeros((1, 4, NT), np.int32)
    meta[0, 0] = tiles % (TOKENS // P) * P
    meta[0, 1] = tiles // (TOKENS // P)
    meta[0, 2] = tiles // (TOKENS // P) % 2 * WCOLS
    arrays = {
        "x": a["x"], "ctxT": a["ctx_1024"].transpose(0, 2, 1), "g_x": a["g_xattn"], "g_f": a["g_ffn"],
        "inT": a["L0_xattn_in_proj_w"].T, "convw": a["L0_xattn_conv_w"], "convb": a["L0_xattn_conv_b"],
        "xpT": xpT, "dtwT": a["L0_xattn_dt_proj_w"].T, "dtb": a["L0_xattn_dt_proj_b"],
        "alog": a["L0_xattn_A_log"], "dvec": a["L0_xattn_D"], "gateT": a["L0_ffn_gate_w"].T, "wall": wall,
        "ident_d": np.eye(P, dtype=np.float32), "iota_d": np.tile(np.arange(DS, dtype=np.float32), (P, 1)),
        "meta_d": meta,
    }
    arrays = {f"in_{k}": np.ascontiguousarray(v) for k, v in arrays.items()}
    nc = bacc.Bacc("TRN2", target_bir_lowering=False, num_devices=1)
    args = [nc.dram_tensor(k, v.shape, mybir.dt.from_np(v.dtype), kind="ExternalInput").ap() for k, v in arrays.items()]
    out = nc.dram_tensor("out_x", (NB, L, H), F32, kind="ExternalOutput").ap()
    mamba_moe(nc, *args, out)
    r = run_bass_kernel_spmd(nc, [arrays], core_ids=[0])
    return r.results[0]["out_x"]
```

```python
from contextlib import ExitStack

import concourse.bass as bass
from concourse import mybir

F32 = mybir.dt.float32
F32R = mybir.dt.float32r
I32 = mybir.dt.int32
U32 = mybir.dt.uint32
ALU = mybir.AluOpType
ACT = mybir.ActivationFunctionType
AX = mybir.AxisListType

P = 128
NB, L, H = 4, 512, 512
DM, DI, DS, DR, DC = 256, 512, 16, 16, 4
J = DI // P
TC = L // P
KC = DM // P
E, TOPK, I = 16, 6, 352
NX = E + 2
HK = H // P
IP = 384
IK = IP // P
WCOLS = HK * 2 * I + IK * H
W2AT = HK * 2 * I
ROW = H + NX + 2
TOKENS = NB * L
TT = TOKENS // P
NS = 2 * TT
NR = TOPK * TT + E
NT = NS + NR
AHEAD = 5
DTP, BP, CP, XP = 0, 32, 64, 80
LN_EPS = 1e-5

PRE_USE = {("inproj", 0): (0, 0), ("inproj", 1): (1, 0), ("inproj", 2): (0, 1), ("inproj", 3): (1, 1),
           ("xproj", 0): (0, 2), ("dt", 0): (1, 2), ("dt", 1): (0, 3), ("bt", 0): (1, 3),
           ("dt", 2): (0, 4), ("dt", 3): (1, 4),
           ("dut", 0): (0, 5), ("dut", 1): (1, 5), ("dut", 2): (0, 6), ("dut", 3): (1, 6)}
EPI_USE = {("yt", 0): (0, 0), ("yt", 1): (1, 0), ("yt", 2): (0, 1), ("yt", 3): (1, 1),
           ("xlt", 0): (0, 2), ("xlt", 1): (1, 2), ("xlt", 2): (0, 3), ("xlt", 3): (1, 3),
           ("logits", 0): (0, 4)}
PRE_N = (7, 7)
EPI_N = (5, 4)


def use(stage, i, q):
    if (stage, i) in PRE_USE:
        bank, m = PRE_USE[(stage, i)]
        return bank, q * (PRE_N[bank] + EPI_N[bank]) + m
    bank, m = EPI_USE[(stage, i)]
    if isinstance(q, int) and q == NB - 1:
        return bank, NB * PRE_N[bank] + (q + 1) * EPI_N[bank] + m
    return bank, (q + 2) * PRE_N[bank] + (q + 1) * EPI_N[bank] + m


def prelude_items(q):
    return {4: [("load", q, 0), ("stats", q, 0), ("inproj", q, 0)], 5: [("inproj", q, 1)],
            6: [("inproj", q, 2)], 7: [("inproj", q, 3)], 8: [("silu", q, 0)], 9: [("xproj", q, 0)],
            10: [("dt", q, 0), ("dt", q, 1)], 11: [("bt", q, 0), ("delta", q, 0), ("delta", q, 1)],
            12: [("dt", q, 2), ("dt", q, 3)], 13: [("delta", q, 2), ("delta", q, 3)],
            14: [("dut", q, 0), ("dut", q, 1)], 15: [("dut", q, 2), ("dut", q, 3)]}


def epilogue_items(b):
    return {0: [("y", b, 0)], 1: [("yt", b, t) for t in range(TC)], 2: [("norm", b, 0)],
            3: [("xlt", b, t) for t in range(TC)] + [("gate", b, 0)]}


def first_part():
    out = [item for n in range(4, DS) for item in prelude_items(0)[n]]
    return out + [("step", 0, n) for n in range(4)]


def batch_part(b, more):
    pre, epi = prelude_items(b + 1), epilogue_items(b)
    out = []
    for n in range(4, DS):
        out.append(("step", b, n))
        if more:
            out += pre[n]
    for n in range(4):
        if more:
            out.append(("step", b + 1, n))
        elif n == 0:
            out.append(("tail", b, 0))
        out += epi[n]
    return out


def mamba_moe(nc, x, ctxT, g_x, g_f, inT, convw, convb, xpT, dtwT, dtb, alog, dvec,
              gateT, wall, ident_d, iota_d, tri_d, ones_d, reset_d, steps_d, tile_d, ids_d, trash_d, out):
    rows_d = nc.dram_tensor("token_rows", (TOKENS + P, ROW), F32, kind="Internal").ap()
    acc_d = nc.dram_tensor("sums", (TOKENS + P, H), F32, kind="Internal").ap()
    list_d = nc.dram_tensor("token_lists", (P * NR, 1), I32, kind="Internal").ap()
    c_d = nc.dram_tensor("c_rows", (NB, DS, L), F32, kind="Internal").ap()
    x_rows = x.rearrange("b (c p) h -> b p c h", p=P)
    acc_v = acc_d[0:TOKENS, :].rearrange("(b c p) h -> b p c h", p=P, c=TC)
    rows_v = rows_d[0:TOKENS, :].rearrange("(b c p) h -> b p c h", p=P, c=TC)

    with ExitStack() as ctx:
        def alloc(stack, name, shape, dt=F32):
            return stack.enter_context(nc.sbuf_tensor(name, shape, dt))

        def sem(name):
            return ctx.enter_context(nc.semaphore(name))

        banks = [ctx.enter_context(nc.psum_tensor(f"bank{i}", [P, 512], F32)) for i in range(8)]
        ysum, dbu, misc = banks[0:4], banks[4:6], banks[6:8]

        ident = alloc(ctx, "ident", [P, P])
        zero = alloc(ctx, "zero", [P, ROW])
        sel = alloc(ctx, "sel", [P, E, TT])
        choice = alloc(ctx, "choice", [P, TT, TOPK])

        mem = ExitStack()
        iota16 = alloc(mem, "iota16", [P, DS])
        inw = alloc(mem, "inw", [P, KC, DI])
        xpw = alloc(mem, "xpw", [P, J, XP])
        dtw = alloc(mem, "dtw", [DR, DI])
        cw = alloc(mem, "cw", [P, J, DC])
        cb = alloc(mem, "cb", [P, J])
        dtbias = alloc(mem, "dtbias", [P, J])
        dsk = alloc(mem, "dsk", [P, J])
        aneg = alloc(mem, "aneg", [P, J, DS])
        aexp = alloc(mem, "aexp", [P, J, DS])
        gx = alloc(mem, "gx", [P, 1])
        gf = alloc(mem, "gf", [P, 1])
        tgx = alloc(mem, "tgx", [P, 1])
        tgf = alloc(mem, "tgf", [P, 1])
        gw = alloc(mem, "gw", [P, HK, E])
        eps = alloc(mem, "eps", [P, 1])
        one = alloc(mem, "one", [P, 1])
        xrow = alloc(mem, "xrow", [P, 2, TC, H])
        ctxt = alloc(mem, "ctxt", [P, KC, L])
        xpad = alloc(mem, "xpad", [P, J, L + 4])
        u = alloc(mem, "u", [P, 2, J, L])
        sz = alloc(mem, "sz", [P, 2, J, L])
        xd = alloc(mem, "xd", [XP, L])
        bst = alloc(mem, "bst", [P, TC, 6])
        bag = alloc(mem, "bag", [P, TC, 2])
        lnv = alloc(mem, "lnv", [P, TC])
        rstd = alloc(mem, "rstd", [P, TC])
        nmr = alloc(mem, "nmr", [P, TC])
        sv = alloc(mem, "sv", [P, 2, L])
        nv = alloc(mem, "nv", [P, 2, L])
        se = alloc(mem, "se", [P, 2, L])
        sw = alloc(mem, "sw", [P, 2, L])
        st1 = alloc(mem, "st1", [P, L])
        st2 = alloc(mem, "st2", [P, L])
        delta = alloc(mem, "delta", [P, 2, J, L])
        du = alloc(mem, "du", [P, J, L])
        y = du
        duT = alloc(mem, "duT", [P, 2, TC, DI])
        btn = alloc(mem, "btn", [P, TC, DS])
        btc = alloc(mem, "btc", [P, TC, DS])
        gt = alloc(mem, "gt", [P, 2, TC, DI])
        dA = alloc(mem, "dA", [P, 4, L])
        hs = alloc(mem, "hs", [P, 4, L])
        crow = alloc(mem, "crow", [P, 4, L])
        hc = alloc(mem, "hc", [P, 4, L])
        bst2 = alloc(mem, "bst2", [P, TC, 6])
        bag2 = alloc(mem, "bag2", [P, TC, 2])
        lnv2 = alloc(mem, "lnv2", [P, TC])
        rstd2 = alloc(mem, "rstd2", [P, TC])
        rowb = alloc(mem, "rowb", [P, TC, ROW])
        xlT = alloc(mem, "xlT", [P, TC, HK, P])
        mx = alloc(mem, "mx", [P, TC])
        lgs = alloc(mem, "lgs", [P, TC, E])
        ex = alloc(mem, "ex", [P, TC, E])
        sm = alloc(mem, "sm", [P, TC])
        rsm = alloc(mem, "rsm", [P, TC])
        sc = alloc(mem, "sc", [P, TC, E])
        m8 = alloc(mem, "m8", [P, TC, 8])
        ix = alloc(mem, "ix", [P, TC, 8], U32)
        ixf = alloc(mem, "ixf", [P, TC, 8])
        eq = alloc(mem, "eq", [P, TC, E, TOPK])
        mask = alloc(mem, "mask", [P, TC, E])
        s6 = alloc(mem, "s6", [P, TC])
        r6 = alloc(mem, "r6", [P, TC])
        r6g = alloc(mem, "r6g", [P, TC])
        mem.close()

        wraw = alloc(ctx, "wraw", [P, WCOLS])
        wh = alloc(ctx, "wh", [P, 2 * WCOLS], F32R)
        wl = alloc(ctx, "wl", [P, 2 * WCOLS], F32R)
        xt = alloc(ctx, "xt", [P, 4, ROW])
        xh = alloc(ctx, "xh", [P, 2, H], F32R)
        xl = alloc(ctx, "xl", [P, 2, H], F32R)
        cc = alloc(ctx, "cc", [P, 2])
        sg = alloc(ctx, "sg", [P, 2, I])
        am = alloc(ctx, "am", [P, 2, IP])
        ah = alloc(ctx, "ah", [P, 2, IP], F32R)
        al = alloc(ctx, "al", [P, 2, IP], F32R)
        ys = alloc(ctx, "ys", [P, 4, H])
        meta = alloc(ctx, "meta", [P, 3, NT], I32)
        ids = alloc(ctx, "ids", [P, NT], I32)
        own = alloc(ctx, "own", [P, TT], I32)
        gid = alloc(ctx, "gid", [P, 4], I32)
        aid = alloc(ctx, "aid", [P, 4], I32)
        tri = alloc(ctx, "tri", [P, P])
        ones = alloc(ctx, "ones", [P, P])
        reset = alloc(ctx, "reset", [P, E, TT])
        steps = alloc(ctx, "steps", [P, TT])
        tileno = alloc(ctx, "tileno", [P, 2, NT])
        iotab = alloc(ctx, "iotab", [P, E])
        total = alloc(ctx, "total", [P, E, TT])
        upto = alloc(ctx, "upto", [P, E, TT])
        over = alloc(ctx, "over", [P, E, TT])
        tiles_e = alloc(ctx, "tiles_e", [P, E])
        one_e = alloc(ctx, "one_e", [P, E])
        end_e = alloc(ctx, "end_e", [P, E])
        first_e = alloc(ctx, "first_e", [P, E])
        rank = alloc(ctx, "rank", [P, E, TT])
        ranki = alloc(ctx, "ranki", [P, E, TT], I32)
        lowi = alloc(ctx, "lowi", [P, E, TT], I32)
        highi = alloc(ctx, "highi", [P, E, TT], I32)
        place = alloc(ctx, "place", [P, E, TT])
        eqb = alloc(ctx, "eqb", [P, TT, TOPK, E])
        posf = alloc(ctx, "posf", [P, TT, TOPK])
        posi = alloc(ctx, "posi", [P, TT * TOPK], I32)
        cur = alloc(ctx, "cur", [P, TOPK], I32)
        curid = alloc(ctx, "curid", [P, 1], I32)
        past = alloc(ctx, "past", [P, NT, E - 1])
        slot = alloc(ctx, "slot", [P, NT])
        sloti = alloc(ctx, "sloti", [P, NT], I32)
        odd = alloc(ctx, "odd", [P, NT], I32)
        fresh = alloc(ctx, "fresh", [P, NT])

        const_in = sem("const_in")
        setup_act = sem("setup_act")
        setup_dve = sem("setup_dve")
        ctx_in = sem("ctx_in")
        xrow_in = sem("xrow_in")
        full = [sem("misc_full0"), sem("misc_full1")]
        gone = [sem("misc_gone0"), sem("misc_gone1")]
        stats_done = sem("stats_done")
        lnv_done = sem("lnv_done")
        rstd_done = sem("rstd_done")
        nmr_done = sem("nmr_done")
        bst_done = sem("bst_done")
        conv_done = sem("conv_done")
        silu_done = sem("silu_done")
        cd_stored = sem("cd_stored")
        crow_in = [sem(f"crow_in{i}") for i in range(4)]
        sv_done = sem("sv_done")
        nv_done = sem("nv_done")
        se_done = sem("se_done")
        sw_done = sem("sw_done")
        st_done = sem("st_done")
        delta_done = sem("delta_done")
        du_done = sem("du_done")
        btc_done = sem("btc_done")
        g_done = sem("g_done")
        turned = sem("turned")
        dA_done = sem("dA_done")
        scanned = sem("scanned")
        hc_done = sem("hc_done")
        summed = sem("summed")
        y_done = sem("y_done")
        yz_done = sem("yz_done")
        x2_done = sem("x2_done")
        bst2_done = sem("bst2_done")
        bag2_done = sem("bag2_done")
        lnv2_done = sem("lnv2_done")
        rstd2_done = sem("rstd2_done")
        norm_done = sem("norm_done")
        base_stored = sem("base_stored")
        rows_stored = sem("rows_stored")
        gate_step = sem("gate_step")
        exp_done = sem("exp_done")
        raw_in = sem("raw_in")
        wh_done = sem("wh_done")
        wl_done = sem("wl_done")
        gathered = sem("gathered")
        zero_done = sem("zero_done")
        blank_in = sem("blank_in")
        plan_in = sem("plan_in")
        sel_done = sem("sel_done")
        counted = sem("counted")
        plan_step = sem("plan_step")
        meta_ready = sem("meta_ready")
        pos_ready = sem("pos_ready")
        listed = sem("listed")
        cur_done = sem("cur_done")
        gid_done = sem("gid_done")
        aid_done = sem("aid_done")
        ids_in = sem("ids_in")
        copied = sem("copied")
        xt_turned = sem("xt_turned")
        xh_done = sem("xh_done")
        xl_done = sem("xl_done")
        cc_done = sem("cc_done")
        up_done = sem("up_done")
        sg_done = sem("sg_done")
        am_done = sem("am_done")
        am_turned = sem("am_turned")
        ah_done = sem("ah_done")
        al_done = sem("al_done")
        down_done = sem("down_done")
        ys_done = sem("ys_done")
        added = sem("added")
        pad_done = sem("pad_done")

        GATE_STEPS = 15
        N_CONST = 13
        N_PLAN = 8
        PLAN_STEPS = 21

        def at_least(eng, s, v):
            if isinstance(v, int) and v <= 0:
                return
            eng.wait_ge(s, v)

        waited = {e: sem(f"waited_{e}") for e in ("sp", "act", "dve", "pe", "pool")}

        def apart(eng, s, v, who):
            at_least(eng, s, v)
            if not isinstance(v, int):
                eng.sem_inc(waited[who], 1)

        block = ctx.enter_context(nc.Block())

        @block.sync
        def _(sp):
            consts = [(ident, ident_d), (iota16, iota_d), (inw, inT.rearrange("(k p) e -> p k e", p=P)),
                      (xpw, xpT.rearrange("(k p) m -> p k m", p=P)), (dtw, dtwT),
                      (cw, convw.rearrange("(j p) c -> p j c", p=P)), (cb, convb.rearrange("(j p) -> p j", p=P)),
                      (dtbias, dtb.rearrange("(j p) -> p j", p=P)), (dsk, dvec.rearrange("(j p) -> p j", p=P)),
                      (aexp, alog.rearrange("(j p) n -> p j n", p=P)), (gw, gateT.rearrange("(k p) e -> p k e", p=P)),
                      (gx, g_x.partition_broadcast(P)), (gf, g_f.partition_broadcast(P))]
            with nc.allow_non_contiguous_dma(reason="per-channel vectors of 512 values"):
                for dst, src in consts:
                    sp.dma_start(dst[:], src).then_inc(const_in, 16)
                sp.wait_ge(zero_done, 1)
                sp.dma_start(rows_d[TOKENS:TOKENS + P, :], zero[:]).then_inc(blank_in, 16)
                sp.dma_start(acc_d[TOKENS:TOKENS + P, :], zero[:, 0:H]).then_inc(blank_in, 16)
                sp.dma_start(list_d.rearrange("(p t) a -> p (t a)", p=P), trash_d).then_inc(blank_in, 16)

            def load(q, _):
                if not (isinstance(q, int) and q == 0):
                    bank, m = use("inproj", 3, q - 1)
                    apart(sp, full[bank], m + 1, "sp")
                    apart(sp, nmr_done, q, "sp")
                    apart(sp, base_stored, 16 * (q - 1), "sp")
                    apart(sp, norm_done, TC * (q - 1), "sp")
                    apart(sp, silu_done, 2 * J * q, "sp")
                sp.dma_start(ctxt[:], ctxT[bass.ds(q, 1)].rearrange("a (k p) t -> p (a k) t", p=P)).then_inc(ctx_in, 16)
                sp.dma_start(xrow[:, bass.ds(q % 2, 1)].rearrange("p a c h -> p (a c) h"),
                             x_rows[bass.ds(q, 1)].rearrange("a p c h -> p (a c) h")).then_inc(xrow_in, 16)

            def xproj(q, _):
                bank, m = use("xproj", 0, q)
                apart(sp, gone[bank], m + 1, "sp")
                sp.dma_start(c_d[bass.ds(q, 1)].rearrange("a n t -> (a n) t"), xd[CP:CP + DS, :]).then_inc(cd_stored, 16)

            def c_row(b, n):
                if n == 0:
                    apart(sp, cd_stored, 16 * (b + 1), "sp")
                apart(sp, hc_done, (b * DS + n - 3) * J, "sp")
                src = c_d[bass.ds(b, 1), n, :].rearrange("a t -> (a t)")
                sp.dma_start(crow[:, n % 4, :], src.partition_broadcast(P)).then_inc(crow_in[n % 4], 16)

            def step(b, n):
                if n + 3 < DS:
                    c_row(b, n + 3)
                elif not (isinstance(b, int) and b == NB - 1):
                    c_row(b + 1, n + 3 - DS)

            def norm(b, _):
                apart(sp, x2_done, TC * (b + 1), "sp")
                sp.dma_start(acc_v[bass.ds(b, 1)].rearrange("a p c h -> p (a c) h"), xrow[:, bass.ds(b % 2, 1)].rearrange("p a c h -> p (a c) h")).then_inc(base_stored, 16)

            def gate(b, _):
                apart(sp, gate_step, GATE_STEPS * (b + 1), "sp")
                apart(sp, norm_done, TC * (b + 1), "sp")
                sp.dma_start(rows_v[bass.ds(b, 1)].rearrange("a p c h -> p (a c) h"), rowb[:]).then_inc(rows_stored, 16)

            work = {"load": load, "xproj": xproj, "step": step, "norm": norm, "gate": gate}

            def run(items):
                for kind, b, i in items:
                    if kind in work:
                        work[kind](b, i)

            ahead = first_part()
            run([item for item in ahead if item[0] != "step"])
            for n in range(3):
                c_row(0, n)
            run([item for item in ahead if item[0] == "step"])
            with sp.Fori(0, NB - 1) as b:
                run(batch_part(b, True))
            run(batch_part(NB - 1, False))

            sp.wait_ge(rows_stored, 16 * NB)
            sp.wait_ge(base_stored, 16 * NB)
            sp.wait_ge(norm_done, TC * NB)
            for dst, src in ((ids[:, 0:NS], ids_d), (own[:], ids_d[:, 0:TT]), (tri[:], tri_d), (ones[:], ones_d),
                             (reset[:], reset_d), (steps[:], steps_d), (tileno[:], tile_d), (iotab[:], iota_d)):
                sp.dma_start(dst, src).then_inc(plan_in, 16)

            def fetch(e):
                at_least(sp, wl_done, e)
                sp.dma_start(wraw[:], wall[bass.ds(e, 1)].rearrange("a p c -> p (a c)")).then_inc(raw_in, 16)

            fetch(0)
            fetch(1)
            fetch(2)
            sp.wait_ge(listed, 16 * TOPK * TT)
            sp.dma_start(ids[:, NS:NT], list_d.rearrange("(p t) a -> p (t a)", p=P)).then_inc(ids_in, 16)
            with sp.Fori(3, NX) as e:
                fetch(e)
            sp.wait_ge(added, 16 * NT)
            sp.dma_start(out.rearrange("b s h -> (b s) h"), acc_d[0:TOKENS, :]).then_inc(copied, 16)
            sp.wait_ge(copied, 16)

        @block.scalar
        def _(act):
            act.wait_ge(const_in, 16 * N_CONST)
            nc.scalar.activation(aneg[:], aexp[:], ACT.Exp).then_inc(setup_act, 1)
            nc.scalar.activation(tgx[:], gx[:], ACT.Tanh).then_inc(setup_act, 1)
            nc.scalar.activation(tgf[:], gf[:], ACT.Tanh).then_inc(setup_act, 1)
            act.wait_ge(setup_dve, 1)

            def evacuate(stage, i, q, dst, cols, parts=P):
                bank, m = use(stage, i, q)
                apart(act, full[bank], m + 1, "act")
                nc.scalar.copy(dst, misc[bank][0:parts, 0:cols]).then_inc(gone[bank], 1)

            def stats(q, _):
                act.wait_ge(stats_done, q + 1)
                at_least(act, nmr_done, q)
                nc.scalar.activation(lnv[:], bag[:, :, 1], ACT.Ln, bias=eps[:]).then_inc(lnv_done, 1)
                act.wait_ge(lnv_done, q + 1)
                at_least(act, silu_done, 2 * J * q)
                nc.scalar.activation(rstd[:], lnv[:], ACT.Exp, scale=-0.5).then_inc(rstd_done, 1)

            def inproj(q, j):
                at_least(act, conv_done, DC * (J * (q - 1) + j + 1) if not (isinstance(q, int) and q == 0) else 0)
                evacuate("inproj", j, q, xpad[:, j, 3:3 + L], L)

            def silu(q, _):
                for j in range(J):
                    apart(act, conv_done, DC * (J * q + j + 1), "act")
                    uj = u[:, bass.ds(q % 2, 1), j, :].rearrange("p a t -> p (a t)")
                    nc.scalar.activation(uj, uj, ACT.Silu, bias=cb[:, j:j + 1]).then_inc(silu_done, 1)
                apart(act, nmr_done, q + 1, "act")
                apart(act, yz_done, J * (q - 1), "act")
                for j in range(J):
                    nc.scalar.activation(sz[:, bass.ds(q % 2, 1), j, :].rearrange("p a t -> p (a t)"),
                                         xrow[:, bass.ds(q % 2, 1), j, :].rearrange("p a t -> p (a t)"),
                                         ACT.Silu, bias=nmr[:, j:j + 1], scale=rstd[:, j:j + 1]).then_inc(silu_done, 1)

            def xproj(q, _):
                at_least(act, cd_stored, 16 * q)
                if not (isinstance(q, int) and q == 0):
                    bank, m = use("dt", 3, q - 1)
                    act.wait_ge(full[bank], m + 1)
                evacuate("xproj", 0, q, xd[:], L, XP)

            def bt(q, _):
                evacuate("bt", 0, q, btn[:].rearrange("p c n -> p (c n)"), TC * DS)

            def dt(q, j):
                act.wait_ge(nv_done, J * q + j + 1)
                at_least(act, st_done, 3 * (J * q + j - 1))
                nc.scalar.activation(se[:, j % 2, :], nv[:, j % 2, :], ACT.Exp).then_inc(se_done, 1)
                act.wait_ge(se_done, J * q + j + 1)
                nc.scalar.activation(sw[:, j % 2, :], se[:, j % 2, :], ACT.Ln, bias=one[:]).then_inc(sw_done, 1)

            def dut(q, t):
                evacuate("dut", t, q, duT[:, bass.ds(q % 2, 1), t, :].rearrange("p a t -> p (a t)"), DI)

            def step(b, n):
                if n == 0:
                    bank, m = use("dut", 3, b)
                    act.wait_ge(gone[bank], m + 1)
                    at_least(act, g_done, DS * b)
                    nc.scalar.copy(btc[:], btn[:]).then_inc(btc_done, 1)
                    apart(act, btc_done, b + 1, "act")
                    bank, m = use("dut", 2, b)
                    apart(act, gone[bank], m + 1, "act")
                    apart(act, delta_done, J * (b + 1), "act")
                apart(act, turned, J * (b * DS + n - 1), "act")
                for t in range(TC):
                    g = nc.scalar.activation(gt[:, n % 2, t, :], duT[:, bass.ds(b % 2, 1), t, :].rearrange("p a t -> p (a t)"),
                                             ACT.Copy, scale=btc[:, t, n:n + 1])
                g.then_inc(g_done, 1)
                for j in range(J):
                    apart(act, scanned, (b * DS + n - 1) * J + j + 1, "act")
                    nc.scalar.activation(dA[:, j, :], delta[:, bass.ds(b % 2, 1), j, :].rearrange("p a t -> p (a t)"),
                                         ACT.Exp, scale=aneg[:, j, n:n + 1]).then_inc(dA_done, 1)

            def norm(b, _):
                act.wait_ge(bag2_done, b + 1)
                at_least(act, norm_done, TC * b)
                nc.scalar.activation(lnv2[:], bag2[:, :, 1], ACT.Ln, bias=eps[:]).then_inc(lnv2_done, 1)
                act.wait_ge(lnv2_done, b + 1)
                nc.scalar.activation(rstd2[:], lnv2[:], ACT.Exp, scale=-0.5).then_inc(rstd2_done, 1)

            def xlt(b, t):
                evacuate("xlt", t, b, xlT[:, t, :, :].rearrange("p k m -> p (k m)"), H)

            def gate(b, _):
                bank, m = use("logits", 0, b)
                act.wait_ge(gone[bank], m + 1)
                nc.scalar.activation(ex[:], lgs[:], ACT.Exp).then_inc(exp_done, 1)

            work = {"stats": stats, "inproj": inproj, "silu": silu, "xproj": xproj, "bt": bt, "dt": dt,
                    "dut": dut, "step": step, "norm": norm, "xlt": xlt, "gate": gate}

            def run(items):
                for kind, b, i in items:
                    if kind in work:
                        work[kind](b, i)

            act.wait_ge(setup_dve, 2)
            run(first_part())
            with act.Fori(0, NB - 1) as b:
                run(batch_part(b, True))
            run(batch_part(NB - 1, False))

            def x_high(t, s):
                act.wait_ge(xt_turned, t + 1)
                at_least(act, up_done, t - 1)
                nc.scalar.copy(xh[:, s, :], banks[0][:]).then_inc(xh_done, 1)

            def gate_up(t, s):
                act.wait_ge(up_done, t + 1)
                at_least(act, am_done, t - 1)
                nc.scalar.activation(sg[:, s, :], banks[1 + 2 * s][:, 0:I], ACT.Silu).then_inc(sg_done, 1)

            def a_high(t, s):
                act.wait_ge(am_turned, t + 1)
                at_least(act, down_done, t - 1)
                nc.scalar.copy(ah[:, s, :], banks[5][:, 0:IP]).then_inc(ah_done, 1)

            def y_out(t, s, slot):
                apart(act, down_done, t + 1, "act")
                apart(act, added, 16 * (t - 3), "act")
                nc.scalar.copy(ys[:, bass.ds(slot, 1), :].rearrange("p a h -> p (a h)"), banks[6 + s][:]).then_inc(ys_done, 1)

            x_high(0, 0)
            x_high(1, 1)
            gate_up(0, 0)
            for t in (1, 2, 3, 4):
                a_high(t - 1, (t - 1) % 2)
                x_high(t + 1, (t + 1) % 2)
                gate_up(t, t % 2)
                y_out(t - 1, (t - 1) % 2, t - 1)
            with act.Fori(2, NT // 2 - 1) as i:
                for k in (1, 2):
                    t, s = 2 * i + k, k % 2
                    a_high(t - 1, 1 - s)
                    x_high(t + 1, 1 - s)
                    gate_up(t, s)
                    y_out(t - 1, 1 - s, (t - 1) % 4)
            a_high(NT - 2, 0)
            gate_up(NT - 1, 1)
            y_out(NT - 2, 0, (NT - 2) % 4)
            a_high(NT - 1, 1)
            y_out(NT - 1, 1, (NT - 1) % 4)

        @block.gpsimd
        def _(pool):
            def step(b, n):
                pool.wait_ge(crow_in[n % 4], 16 * (b * (DS // 4) + n // 4 + 1))
                for j in range(J):
                    i = (b * DS + n) * J + j
                    pool.wait_ge(scanned, i + 1)
                    at_least(pool, summed, i - 3)
                    nc.gpsimd.tensor_tensor(hc[:, j, :], hs[:, j, :], crow[:, n % 4, :], ALU.mult).then_inc(hc_done, 1)

            def run(items):
                for kind, b, n in items:
                    if kind == "step":
                        step(b, n)

            run(first_part())
            with pool.Fori(0, NB - 1) as b:
                run(batch_part(b, True))
            run(batch_part(NB - 1, False))

            pool.wait_ge(rows_stored, 16 * NB)
            pool.wait_ge(base_stored, 16 * NB)

            pool.wait_ge(blank_in, 48)

            def split(e, t):
                half = bass.ds((e % 2) * WCOLS, WCOLS)
                apart(pool, raw_in, 16 * (e + 1), "pool")
                apart(pool, down_done, t, "pool")
                nc.gpsimd.tensor_copy(wh[:, half], wraw[:]).then_inc(wh_done, 1)
                apart(pool, wh_done, e + 1, "pool")
                nc.gpsimd.tensor_tensor(wl[:, half], wraw[:], wh[:, half], ALU.subtract).then_inc(wl_done, 1)

            def gather(t, s):
                apart(pool, xt_turned, t - 3, "pool")
                apart(pool, cc_done, t - 3, "pool")
                apart(pool, gathered, 16 * t, "pool")
                nc.gpsimd.tensor_copy(gid[:, s:s + 1], ids[:, bass.ds(t, 1)]).then_inc(gid_done, 1)
                apart(pool, gid_done, t + 1, "pool")
                pool.indirect_dma_start(xt[:, s, :], None, rows_d[:, :], bass.IndirectOffsetOnAxis(ap=gid[:, s:s + 1], axis=0)).then_inc(gathered, 16)

            def add(t, s):
                apart(pool, ys_done, t + 1, "pool")
                apart(pool, added, 16 * t, "pool")
                nc.gpsimd.tensor_copy(aid[:, s:s + 1], ids[:, bass.ds(t, 1)]).then_inc(aid_done, 1)
                apart(pool, aid_done, t + 1, "pool")
                pool.indirect_dma_start(acc_d[:, :], bass.IndirectOffsetOnAxis(ap=aid[:, s:s + 1], axis=0), ys[:, s, :], None,
                                        compute_op=ALU.add).then_inc(added, 16)

            def list_tokens(c):
                apart(pool, listed, 16 * TOPK * c, "pool")
                nc.gpsimd.tensor_copy(cur[:], posi[:, bass.ds(c * TOPK, TOPK)]).then_inc(cur_done, 1)
                nc.gpsimd.tensor_copy(curid[:], own[:, bass.ds(c, 1)]).then_inc(cur_done, 1)
                apart(pool, cur_done, 2 * (c + 1), "pool")
                for k in range(TOPK):
                    pool.indirect_dma_start(list_d[:, :], bass.IndirectOffsetOnAxis(ap=cur[:, k:k + 1], axis=0), curid[:], None).then_inc(listed, 16)

            def next_weights(t):
                e = pool.value_load(meta[0:1, 2, bass.ds(t, 1)], min_val=0, max_val=NX - 1)
                with pool.If(e > 0):
                    split(e, t)

            pool.wait_ge(plan_in, 16 * N_PLAN)
            for t in range(4):
                gather(t, t)
            split(0, 0)
            split(1, 0)
            gather(4, 0)
            pool.wait_ge(meta_ready, 1)
            pool.wait_ge(pos_ready, 1)
            for t in range(4):
                gather(t + AHEAD, (t + AHEAD) % 4)
                add(t, t)
                list_tokens(t)
            with pool.Fori(1, TT // 4) as i:
                for k in range(4):
                    gather(4 * i + k + AHEAD, (k + AHEAD) % 4)
                    add(4 * i + k, k)
                    list_tokens(4 * i + k)
            with pool.Fori(TT // 4, TT // 4 + 2) as i:
                for k in range(4):
                    gather(4 * i + k + AHEAD, (k + AHEAD) % 4)
                    next_weights(4 * i + k)
                    add(4 * i + k, k)
            pool.wait_ge(ids_in, 16)
            with pool.Fori(TT // 4 + 2, NT // 4 - 2) as i:
                for k in range(4):
                    gather(4 * i + k + AHEAD, (k + AHEAD) % 4)
                    next_weights(4 * i + k)
                    add(4 * i + k, k)
            for t in range(NT - 8, NT):
                if t + AHEAD < NT:
                    gather(t + AHEAD, (t + AHEAD) % 4)
                next_weights(t)
                add(t, t % 4)

        @block.vector
        def _(dve):
            nc.vector.memset(eps[:], LN_EPS)
            nc.vector.memset(one[:], 1.0)
            nc.vector.memset(xpad[:], 0.0).then_inc(setup_dve, 1)
            dve.wait_ge(setup_act, 3)
            nc.vector.tensor_scalar(aneg[:], aneg[:], -1.0, None, ALU.mult).then_inc(setup_dve, 1)
            nc.vector.memset(zero[:], 0.0).then_inc(zero_done, 1)
            nc.vector.memset(rowb[:], 1.0).then_inc(setup_dve, 1)
            dve.wait_ge(setup_dve, 3)
            nc.vector.tensor_scalar(rowb[:, :, H:H + 2], rowb[:, :, H:H + 2], tgf[:, 0:1], None,
                                    ALU.mult).then_inc(setup_dve, 1)

            def stats(q, _):
                apart(dve, xrow_in, 16 * (q + 1), "dve")
                apart(dve, stats_done, q, "dve")
                for c in range(TC):
                    nc.vector.bn_stats(bst[:, c, :], xrow[:, bass.ds(q % 2, 1), c, :].rearrange("p a h -> p (a h)")).then_inc(bst_done, 1)
                apart(dve, bst_done, TC * (q + 1), "dve")
                apart(dve, nmr_done, q, "dve")
                for c in range(TC):
                    ins = nc.vector.bn_aggr(bag[:, c, :], bst[:, c, :])
                ins.then_inc(stats_done, 1)
                dve.wait_ge(rstd_done, q + 1)
                dve.wait_ge(stats_done, q + 1)
                at_least(dve, silu_done, 2 * J * q)
                nc.vector.scalar_tensor_tensor(out=nmr[:], in0=bag[:, :, 0], scalar=-1.0, in1=rstd[:],
                                               op0=ALU.mult, op1=ALU.mult).then_inc(nmr_done, 1)

            def inproj(q, j):
                bank, m = use("inproj", j, q)
                dve.wait_ge(gone[bank], m + 1)
                if j == 0:
                    at_least(dve, y_done, J * (q - 1))
                uj = u[:, bass.ds(q % 2, 1), j, :].rearrange("p a t -> p (a t)")
                nc.vector.tensor_scalar(uj, xpad[:, j, 3:3 + L], cw[:, j, 3:4], None, ALU.mult).then_inc(conv_done, 1)
                for k in (2, 1, 0):
                    dve.wait_ge(conv_done, DC * (J * q + j) + 3 - k)
                    nc.vector.scalar_tensor_tensor(out=uj, in0=xpad[:, j, k:k + L], scalar=cw[:, j, k:k + 1], in1=uj,
                                                   op0=ALU.mult, op1=ALU.add).then_inc(conv_done, 1)

            def dt(q, j):
                bank, m = use("dt", j, q)
                dve.wait_ge(full[bank], m + 1)
                at_least(dve, delta_done, J * q + j - 1)
                nc.vector.tensor_scalar(sv[:, j % 2, :], misc[bank][:], dtbias[:, j:j + 1], None, ALU.add).then_inc(gone[bank], 1)
                dve.wait_ge(gone[bank], m + 1)
                nc.vector.scalar_tensor_tensor(out=nv[:, j % 2, :], in0=sv[:, j % 2, :], scalar=-1.0, in1=sv[:, j % 2, :],
                                               op0=ALU.mult, op1=ALU.min).then_inc(nv_done, 1)

            def delta_(q, j):
                i = J * q + j
                dve.wait_ge(sw_done, i + 1)
                at_least(dve, st_done, 3 * i)
                nc.vector.tensor_scalar(st1[:], se[:, j % 2, :], 1.0, -1.0, ALU.add, ALU.add).then_inc(st_done, 1)
                dve.wait_ge(st_done, 3 * i + 1)
                nc.vector.tensor_tensor(st2[:], se[:, j % 2, :], st1[:], ALU.subtract).then_inc(st_done, 1)
                dve.wait_ge(st_done, 3 * i + 2)
                nc.vector.tensor_tensor(st1[:], sw[:, j % 2, :], st2[:], ALU.add).then_inc(st_done, 1)
                dve.wait_ge(st_done, 3 * i + 3)
                if j == 0:
                    at_least(dve, dA_done, (q - 1) * DS * J)
                dj = delta[:, bass.ds(q % 2, 1), j, :].rearrange("p a t -> p (a t)")
                nc.vector.scalar_tensor_tensor(out=dj, in0=sv[:, j % 2, :], scalar=0.0, in1=st1[:],
                                               op0=ALU.max, op1=ALU.add).then_inc(delta_done, 1)
                dve.wait_ge(delta_done, i + 1)
                dve.wait_ge(silu_done, 2 * J * q + j + 1)
                if not (isinstance(q, int) and q == 0):
                    bank, m = use("yt", 3, q - 2)
                    dve.wait_ge(full[bank], m + 1)
                nc.vector.tensor_tensor(du[:, j, :], dj, u[:, bass.ds(q % 2, 1), j, :].rearrange("p a t -> p (a t)"),
                                        ALU.mult).then_inc(du_done, 1)

            def step(b, n):
                for j in range(J):
                    i = (b * DS + n) * J + j
                    dve.wait_ge(dA_done, i + 1)
                    dve.wait_ge(turned, i + 1)
                    at_least(dve, hc_done, i - 3)
                    nc.vector.tensor_tensor_scan(hs[:, j, :], dA[:, j, :], dbu[j % 2][:], 0.0,
                                                 ALU.mult, ALU.add).then_inc(scanned, 1)

            def y_(b, _):
                bank, m = use("dut", 3, b if isinstance(b, int) and b == NB - 1 else b + 1)
                dve.wait_ge(full[bank], m + 1)
                for j in range(J):
                    dve.wait_ge(summed, ((b + 1) * DS - 1) * J + j + 1)
                    nc.vector.scalar_tensor_tensor(out=y[:, j, :], in0=u[:, bass.ds(b % 2, 1), j, :].rearrange("p a t -> p (a t)"),
                                                   scalar=dsk[:, j:j + 1], in1=ysum[j][:],
                                                   op0=ALU.mult, op1=ALU.add).then_inc(y_done, 1)
                for j in range(J):
                    dve.wait_ge(y_done, J * b + j + 1)
                    nc.vector.tensor_tensor(y[:, j, :], y[:, j, :], sz[:, bass.ds(b % 2, 1), j, :].rearrange("p a t -> p (a t)"),
                                            ALU.mult).then_inc(yz_done, 1)

            def yt(b, t):
                bank, m = use("yt", t, b)
                dve.wait_ge(full[bank], m + 1)
                if t == 0:
                    dve.wait_ge(silu_done, 2 * J * (b + 1))
                x2 = xrow[:, bass.ds(b % 2, 1), t, :].rearrange("p a h -> p (a h)")
                nc.vector.scalar_tensor_tensor(out=x2, in0=misc[bank][:], scalar=tgx[:, 0:1],
                                               in1=x2,
                                               op0=ALU.mult, op1=ALU.add).then_inc(gone[bank], 1)
                apart(dve, gone[bank], m + 1, "dve")
                apart(dve, bag2_done, b, "dve")
                nc.vector.bn_stats(bst2[:, t, :], x2).then_inc(x2_done, 1)

            def norm(b, _):
                apart(dve, x2_done, TC * (b + 1), "dve")
                for t in range(TC):
                    ins = nc.vector.bn_aggr(bag2[:, t, :], bst2[:, t, :])
                ins.then_inc(bag2_done, 1)
                dve.wait_ge(bag2_done, b + 1)
                dve.wait_ge(rstd2_done, b + 1)
                at_least(dve, rows_stored, 16 * b)
                for t in range(TC):
                    x2 = xrow[:, bass.ds(b % 2, 1), t, :].rearrange("p a h -> p (a h)")
                    nc.vector.tensor_scalar(rowb[:, t, 0:H], x2, bag2[:, t, 0:1], rstd2[:, t:t + 1],
                                            ALU.subtract, ALU.mult).then_inc(norm_done, 1)

            def gate(b, _):
                done = [0]
                steps = GATE_STEPS * b

                def chained(ins):
                    ins.then_inc(gate_step, 1)
                    done[0] += 1
                    apart(dve, gate_step, steps + done[0], "dve")

                bank, m = use("logits", 0, b)
                logits = misc[bank][:, 0:TC * E].rearrange("p (c e) -> p c e", e=E)
                dve.wait_ge(full[bank], m + 1)
                chained(nc.vector.tensor_reduce(mx[:], logits, AX.X, ALU.max))
                nc.vector.tensor_tensor(lgs[:], logits, mx[:].unsqueeze(2).to_broadcast([P, TC, E]),
                                        ALU.subtract).then_inc(gone[bank], 1)
                dve.wait_ge(exp_done, b + 1)
                chained(nc.vector.tensor_reduce(sm[:], ex[:], AX.X, ALU.add))
                chained(nc.vector.reciprocal(rsm[:], sm[:]))
                chained(nc.vector.tensor_tensor(sc[:], ex[:], rsm[:].unsqueeze(2).to_broadcast([P, TC, E]), ALU.mult))
                for t in range(TC):
                    ins = nc.vector.max(m8[:, t, :], sc[:, t, :])
                chained(ins)
                for t in range(TC):
                    ins = nc.vector.max_index(ix[:, t, :], m8[:, t, :], sc[:, t, :])
                chained(ins)
                chained(nc.vector.tensor_copy(ixf[:], ix[:]))
                chained(nc.vector.tensor_tensor(
                    eq[:], iota16[:].unsqueeze(1).unsqueeze(3).to_broadcast([P, TC, E, TOPK]),
                    ixf[:, :, 0:TOPK].unsqueeze(2).to_broadcast([P, TC, E, TOPK]), ALU.is_equal))
                chained(nc.vector.tensor_reduce(mask[:], eq[:], AX.X, ALU.add))
                nc.vector.tensor_copy(sel[:, :, bass.ds(b * TC, TC)].rearrange("p e c -> p c e"), mask[:]).then_inc(sel_done, 1)
                nc.vector.tensor_copy(choice[:, bass.ds(b * TC, TC), :], ixf[:, :, 0:TOPK]).then_inc(sel_done, 1)
                chained(nc.vector.tensor_tensor(sc[:], mask[:], sc[:], ALU.mult))
                chained(nc.vector.tensor_reduce(s6[:], m8[:, :, 0:TOPK], AX.X, ALU.add))
                chained(nc.vector.tensor_scalar(s6[:], s6[:], 1e-20, None, ALU.add))
                chained(nc.vector.reciprocal(r6[:], s6[:]))
                chained(nc.vector.tensor_scalar(r6g[:], r6[:], tgf[:, 0:1], None, ALU.mult))
                chained(nc.vector.tensor_tensor(rowb[:, :, H + 2:H + NX], sc[:], r6g[:].unsqueeze(2).to_broadcast([P, TC, E]), ALU.mult))
                assert done[0] == GATE_STEPS

            work = {"stats": stats, "inproj": inproj, "dt": dt, "delta": delta_, "step": step, "y": y_, "yt": yt,
                    "norm": norm, "gate": gate}

            def run(items):
                for kind, b, i in items:
                    if kind in work:
                        work[kind](b, i)

            run(first_part())
            with dve.Fori(0, NB - 1) as b:
                run(batch_part(b, True))
            run(batch_part(NB - 1, False))

            dve.wait_ge(rows_stored, 16 * NB)
            dve.wait_ge(base_stored, 16 * NB)
            nc.vector.memset(am[:], 0.0).then_inc(pad_done, 1)
            nc.vector.memset(one_e[:], 1.0).then_inc(pad_done, 1)
            dve.wait_ge(pad_done, 2)

            done = [0]

            def chained(ins):
                ins.then_inc(plan_step, 1)
                done[0] += 1
                dve.wait_ge(plan_step, done[0])

            def all_of(a):
                return a.rearrange("p e c -> p (e c)")

            dve.wait_ge(plan_in, 16 * N_PLAN)
            dve.wait_ge(counted, 1)
            chained(nc.vector.tensor_copy(all_of(total[:]), banks[0][:, 0:E * TT]))
            chained(nc.vector.tensor_tensor_scan(all_of(upto[:]), all_of(reset[:]), all_of(total[:]), 0.0, ALU.mult, ALU.add))
            chained(nc.vector.tensor_tensor(over[:], upto[:, :, TT - 1:TT].to_broadcast([P, E, TT]),
                                            steps[:].unsqueeze(1).to_broadcast([P, E, TT]), ALU.is_gt))
            chained(nc.vector.tensor_reduce(tiles_e[:], over[:], AX.X, ALU.add))
            chained(nc.vector.tensor_scalar(tiles_e[:], tiles_e[:], 1.0, None, ALU.max))
            chained(nc.vector.tensor_tensor_scan(end_e[:], one_e[:], tiles_e[:], float(NS), ALU.mult, ALU.add))
            chained(nc.vector.tensor_tensor(past[:], tileno[:, 0, :].unsqueeze(2).to_broadcast([P, NT, E - 1]),
                                            end_e[:, 0:E - 1].unsqueeze(1).to_broadcast([P, NT, E - 1]), ALU.is_ge))
            chained(nc.vector.tensor_reduce(slot[:], past[:], AX.X, ALU.add))
            chained(nc.vector.tensor_tensor(slot[:], slot[:], tileno[:, 1, :], ALU.add))
            chained(nc.vector.tensor_scalar(meta[:, 0, :], slot[:], 1.0, None, ALU.add))
            chained(nc.vector.tensor_copy(sloti[:], slot[:]))
            chained(nc.vector.tensor_scalar(odd[:], sloti[:], 1, None, ALU.bitwise_and))
            chained(nc.vector.tensor_scalar(meta[:, 1, :], odd[:], float(WCOLS), None, ALU.mult))
            chained(nc.vector.tensor_tensor(fresh[:, 1:NT], slot[:, 1:NT], slot[:, 0:NT - 1], ALU.subtract))
            nc.vector.memset(fresh[:, 0:1], 0.0).then_inc(pad_done, 1)
            dve.wait_ge(pad_done, 3)
            chained(nc.vector.scalar_tensor_tensor(out=fresh[:], in0=slot[:], scalar=float(NX - 1), in1=fresh[:],
                                                   op0=ALU.is_lt, op1=ALU.mult))
            nc.vector.scalar_tensor_tensor(out=meta[:, 2, :], in0=slot[:], scalar=1.0, in1=fresh[:],
                                           op0=ALU.add, op1=ALU.mult).then_inc(meta_ready, 1)

            chained(nc.vector.tensor_tensor(rank[:], upto[:], total[:], ALU.subtract))
            chained(nc.vector.tensor_tensor(all_of(ranki[:]), all_of(rank[:]), banks[1][:, 0:E * TT], ALU.add))
            nc.vector.tensor_scalar(highi[:], ranki[:], 7, None, ALU.arith_shift_right).then_inc(pad_done, 1)
            chained(nc.vector.tensor_scalar(lowi[:], ranki[:], P - 1, None, ALU.bitwise_and))
            dve.wait_ge(pad_done, 4)
            chained(nc.vector.scalar_tensor_tensor(out=place[:], in0=lowi[:], scalar=float(NR), in1=highi[:],
                                                   op0=ALU.mult, op1=ALU.add))
            chained(nc.vector.scalar_tensor_tensor(out=first_e[:], in0=end_e[:], scalar=float(NS), in1=tiles_e[:],
                                                   op0=ALU.subtract, op1=ALU.subtract))
            chained(nc.vector.tensor_tensor(place[:], place[:], first_e[:].unsqueeze(2).to_broadcast([P, E, TT]), ALU.add))
            assert done[0] == PLAN_STEPS
            nc.vector.tensor_tensor(eqb[:], choice[:].unsqueeze(3).to_broadcast([P, TT, TOPK, E]),
                                    iotab[:].unsqueeze(1).unsqueeze(1).to_broadcast([P, TT, TOPK, E]), ALU.is_equal).then_inc(pad_done, 1)
            dve.wait_ge(pad_done, 5)
            nc.vector.tensor_tensor(eqb[:], eqb[:], place[:].rearrange("p e c -> p c e").unsqueeze(2).to_broadcast([P, TT, TOPK, E]),
                                    ALU.mult).then_inc(pad_done, 1)
            dve.wait_ge(pad_done, 6)
            nc.vector.tensor_reduce(posf[:], eqb[:], AX.X, ALU.add).then_inc(pad_done, 1)
            dve.wait_ge(pad_done, 7)
            nc.vector.tensor_copy(posi[:], posf[:].rearrange("p c k -> p (c k)")).then_inc(pos_ready, 1)
            dve.wait_ge(meta_ready, 1)

            def x_low(t, s):
                dve.wait_ge(xh_done, t + 1)
                at_least(dve, up_done, t - 1)
                nc.vector.tensor_tensor(xl[:, s, :], banks[0][:], xh[:, s, :], ALU.subtract).then_inc(xl_done, 1)

            def take_weight(t, s4):
                e = dve.value_load(meta[0:1, 0, bass.ds(t, 1)], min_val=1, max_val=NX)
                apart(dve, gathered, 16 * (t + 1), "dve")
                at_least(dve, am_done, t - 1)
                nc.vector.tensor_copy(cc[:, s4 % 2:s4 % 2 + 1], xt[:, s4, bass.ds(H - 1 + e, 1)]).then_inc(cc_done, 1)

            def multiply(t, s):
                dve.wait_ge(sg_done, t + 1)
                dve.wait_ge(cc_done, t + 1)
                at_least(dve, am_turned, t - 1)
                nc.vector.scalar_tensor_tensor(out=am[:, s, 0:I], in0=sg[:, s, :], scalar=cc[:, s:s + 1],
                                               in1=banks[2 + 2 * s][:, 0:I], op0=ALU.mult, op1=ALU.mult).then_inc(am_done, 1)

            def a_low(t, s):
                dve.wait_ge(ah_done, t + 1)
                at_least(dve, down_done, t - 1)
                nc.vector.tensor_tensor(al[:, s, :], banks[5][:, 0:IP], ah[:, s, :], ALU.subtract).then_inc(al_done, 1)

            def tile(t, s4):
                s = s4 % 2
                a_low(t - 1, 1 - s)
                take_weight(t + 1, (s4 + 1) % 4)
                x_low(t + 1, 1 - s)
                multiply(t, s)

            take_weight(0, 0)
            x_low(0, 0)
            take_weight(1, 1)
            x_low(1, 1)
            multiply(0, 0)
            tile(1, 1)
            tile(2, 2)
            with dve.Fori(0, NT // 4 - 1) as i:
                for k in range(4):
                    tile(4 * i + 3 + k, (3 + k) % 4)
            a_low(NT - 2, 0)
            multiply(NT - 1, 1)
            a_low(NT - 1, 1)

        @block.tensor
        def _(pe):
            pe.wait_ge(const_in, 16 * N_CONST)

            def claim(stage, i, q, held=False):
                bank, m = use(stage, i, q)
                if held:
                    apart(pe, gone[bank], m, "pe")
                else:
                    at_least(pe, gone[bank], m)
                return misc[bank], full[bank]

            def inproj(q, j):
                pe.wait_ge(ctx_in, 16 * (q + 1))
                bank, done = claim("inproj", j, q)
                for k in range(KC):
                    mm = nc.tensor.matmul(bank[:], inw[:, k, j * P:(j + 1) * P], ctxt[:, k, :], start=k == 0, stop=k == KC - 1)
                mm.then_inc(done, 1)

            def xproj(q, _):
                pe.wait_ge(silu_done, 2 * J * q + J)
                bank, done = claim("xproj", 0, q)
                for k in range(J):
                    mm = nc.tensor.matmul(bank[0:XP, :], xpw[:, k, :], u[:, bass.ds(q % 2, 1), k, :].rearrange("p a t -> p (a t)"),
                                          start=k == 0, stop=k == J - 1)
                mm.then_inc(done, 1)

            def dt(q, j):
                if j == 0:
                    xb, xm = use("xproj", 0, q)
                    pe.wait_ge(gone[xb], xm + 1)
                bank, done = claim("dt", j, q)
                nc.tensor.matmul(bank[:], dtw[:, j * P:(j + 1) * P], xd[DTP:DTP + DR, :], start=True, stop=True).then_inc(done, 1)

            def bt(q, _):
                bank, done = claim("bt", 0, q, True)
                if not (isinstance(q, int) and q == 0):
                    apart(pe, btc_done, q, "pe")
                for t in range(TC):
                    mm = nc.tensor.transpose(bank[:, t * DS:(t + 1) * DS], xd[BP:BP + DS, t * P:(t + 1) * P], ident[BP:BP + DS, BP:BP + DS])
                mm.then_inc(done, 1)

            def dut(q, t):
                pe.wait_ge(du_done, J * (q + 1))
                bank, done = claim("dut", t, q)
                for j in range(J):
                    mm = nc.tensor.transpose(bank[:, j * P:(j + 1) * P], du[:, j, t * P:(t + 1) * P], ident[:])
                mm.then_inc(done, 1)

            def add_products(b, n):
                for j in range(J):
                    pe.wait_ge(hc_done, (b * DS + n) * J + j + 1)
                    if n == 0:
                        at_least(pe, y_done, J * (b - 1) + j + 1)
                    nc.tensor.matmul(ysum[j][:], ident[:], hc[:, j, :], start=n == 0, stop=n == DS - 1,
                                     skip_group_check=True).then_inc(summed, 1)

            def step(b, n):
                pe.wait_ge(g_done, b * DS + n + 1)
                for j in range(J):
                    at_least(pe, scanned, (b * DS + n) * J + j - 1)
                    for t in range(TC):
                        mm = nc.tensor.transpose(dbu[j % 2][:, t * P:(t + 1) * P], gt[:, n % 2, t, j * P:(j + 1) * P], ident[:])
                    mm.then_inc(turned, 1)
                if n > 0:
                    add_products(b, n - 1)
                elif not (isinstance(b, int) and b == 0):
                    add_products(b - 1, DS - 1)

            def tail(b, _):
                add_products(b, DS - 1)

            def yt(b, t):
                pe.wait_ge(yz_done, J * (b + 1))
                bank, done = claim("yt", t, b)
                for j in range(J):
                    mm = nc.tensor.transpose(bank[:, j * P:(j + 1) * P], y[:, j, t * P:(t + 1) * P], ident[:])
                mm.then_inc(done, 1)

            def xlt(b, t):
                pe.wait_ge(norm_done, TC * b + t + 1)
                bank, done = claim("xlt", t, b)
                for k in range(HK):
                    mm = nc.tensor.transpose(bank[:, k * P:(k + 1) * P], rowb[:, t, k * P:(k + 1) * P], ident[:])
                mm.then_inc(done, 1)

            def gate(b, _):
                xb, xm = use("xlt", 3, b)
                pe.wait_ge(gone[xb], xm + 1)
                bank, done = claim("logits", 0, b)
                for t in range(TC):
                    for k in range(HK):
                        mm = nc.tensor.matmul(bank[:, t * E:(t + 1) * E], xlT[:, t, k, :], gw[:, k, :],
                                              start=k == 0, stop=k == HK - 1)
                mm.then_inc(done, 1)

            work = {"inproj": inproj, "xproj": xproj, "bt": bt, "dt": dt, "dut": dut, "step": step, "tail": tail,
                    "yt": yt, "xlt": xlt, "gate": gate}

            def run(items):
                for kind, b, i in items:
                    if kind in work:
                        work[kind](b, i)

            run(first_part())
            for k in range(2):
                pe.wait_ge(gone[k], PRE_N[k])
                pe.sem_inc(full[k], EPI_N[k])
                pe.sem_inc(gone[k], EPI_N[k])
            with pe.Fori(0, NB - 1) as b:
                run(batch_part(b, True))
            run(batch_part(NB - 1, False))

            pe.wait_ge(rows_stored, 16 * NB)
            pe.wait_ge(sel_done, 2 * NB)
            pe.wait_ge(plan_in, 16 * N_PLAN)
            nc.tensor.matmul(banks[1][:, 0:E * TT], tri[:], sel[:].rearrange("p e c -> p (e c)"), start=True, stop=True)
            nc.tensor.matmul(banks[0][:, 0:E * TT], ones[:], sel[:].rearrange("p e c -> p (e c)"), start=True, stop=True).then_inc(counted, 1)
            pe.wait_ge(pos_ready, 1)
            pe.wait_ge(meta_ready, 1)

            def turn_x(t, s):
                apart(pe, gathered, 16 * (t + 1), "pe")
                at_least(pe, xl_done, t)
                for k in range(HK):
                    mm = nc.tensor.transpose(banks[0][:, k * P:(k + 1) * P], xt[:, s, k * P:(k + 1) * P], ident[:])
                mm.then_inc(xt_turned, 1)

            def up(t, s, chunks, off):
                gate_bank, up_bank = banks[1 + 2 * s], banks[2 + 2 * s]
                if chunks[0] == 0:
                    pe.wait_ge(xl_done, t + 1)
                    at_least(pe, am_done, t - 1)
                for k in chunks:
                    high, low = xh[:, s, k * P:(k + 1) * P], xl[:, s, k * P:(k + 1) * P]
                    for n, (xx, ww) in enumerate(((high, wh), (high, wl), (low, wh))):
                        first, last = k == 0 and n == 0, k == HK - 1 and n == 2
                        nc.tensor.matmul(gate_bank[:, 0:I], xx, ww[:, bass.ds(off + k * 2 * I, I)], start=first, stop=last)
                        mm = nc.tensor.matmul(up_bank[:, 0:I], xx, ww[:, bass.ds(off + k * 2 * I + I, I)], start=first, stop=last)
                if chunks[-1] == HK - 1:
                    mm.then_inc(up_done, 1)

            def turn_a(t, s):
                pe.wait_ge(am_done, t + 1)
                at_least(pe, al_done, t)
                for k in range(IK):
                    mm = nc.tensor.transpose(banks[5][:, k * P:(k + 1) * P], am[:, s, k * P:(k + 1) * P], ident[:])
                mm.then_inc(am_turned, 1)

            def down(t, s, off):
                pe.wait_ge(al_done, t + 1)
                at_least(pe, ys_done, t - 1)
                for k in range(IK):
                    high, low = ah[:, s, k * P:(k + 1) * P], al[:, s, k * P:(k + 1) * P]
                    for n, (aa, ww) in enumerate(((high, wh), (high, wl), (low, wh))):
                        mm = nc.tensor.matmul(banks[6 + s][:], aa, ww[:, bass.ds(off + W2AT + k * H, H)],
                                              start=k == 0 and n == 0, stop=k == IK - 1 and n == 2)
                mm.then_inc(down_done, 1)

            def weights_of(t):
                needed = pe.value_load(meta[0:1, 0, bass.ds(t, 1)], min_val=1, max_val=NX)
                apart(pe, wl_done, needed, "pe")
                return pe.value_load(meta[0:1, 1, bass.ds(t, 1)], min_val=0, max_val=WCOLS)

            def tile(t, s4, old, off, more=True):
                s = s4 % 2
                up(t, s, (0, 1), off)
                turn_a(t - 1, 1 - s)
                up(t, s, (2, 3), off)
                if more:
                    turn_x(t + 1, (s4 + 1) % 4)
                down(t - 1, 1 - s, old)

            turn_x(0, 0)
            turn_x(1, 1)
            first = weights_of(0)
            up(0, 0, (0, 1, 2, 3), first)
            second = weights_of(1)
            tile(1, 1, first, second)
            third = weights_of(2)
            tile(2, 2, second, third)
            with pe.Fori(0, NT // 4 - 1) as i:
                old = pe.value_load(meta[0:1, 1, bass.ds(4 * i + 2, 1)], min_val=0, max_val=WCOLS)
                for k in range(4):
                    off = weights_of(4 * i + 3 + k)
                    tile(4 * i + 3 + k, (3 + k) % 4, old, off)
                    old = off
            old = pe.value_load(meta[0:1, 1, NT - 2:NT - 1], min_val=0, max_val=WCOLS)
            tile(NT - 1, (NT - 1) % 4, old, weights_of(NT - 1), False)
            turn_a(NT - 1, 1)
            down(NT - 1, 1, pe.value_load(meta[0:1, 1, NT - 1:NT], min_val=0, max_val=WCOLS))


def kernel(**inputs):
    import numpy as np
    import concourse.bacc as bacc
    from concourse.bass_utils import run_bass_kernel_spmd

    a = {k: np.asarray(v) for k, v in inputs.items()}
    f = a["x"].dtype
    xp = a["L0_xattn_x_proj_w"]
    xpT = np.zeros((DI, XP), f)
    xpT[:, DTP:DTP + DR] = xp[:DR].T
    xpT[:, BP:BP + DS] = xp[DR:DR + DS].T
    xpT[:, CP:CP + DS] = xp[DR + DS:].T
    s13, s2 = a["L0_ffn_sw13"], a["L0_ffn_sw2"]
    w13 = np.concatenate([np.stack([np.concatenate([s13[I * i:I * i + I], s13[2 * I + I * i:3 * I + I * i]]) for i in range(2)]), a["L0_ffn_w13"]])
    w2 = np.concatenate([np.stack([s2[:, I * i:I * i + I] for i in range(2)]), a["L0_ffn_w2"]])
    wall = np.zeros((NX, P, WCOLS), f)
    wall[:, :, :W2AT] = w13.transpose(0, 2, 1).reshape(NX, HK, P, 2 * I).transpose(0, 2, 1, 3).reshape(NX, P, W2AT)
    w2p = np.zeros((NX, IP, H), f)
    w2p[:, :I] = w2.transpose(0, 2, 1)
    wall[:, :, W2AT:] = w2p.reshape(NX, IK, P, H).transpose(0, 2, 1, 3).reshape(NX, P, IK * H)
    part, tiles = np.arange(P, dtype=np.int32)[:, None], np.arange(NT)
    reset = np.ones((P, E, TT), np.float32)
    reset[:, :, 0] = 0
    number = np.stack([tiles, np.minimum(tiles // TT, 2)]).astype(np.float32)
    arrays = {
        "x": a["x"], "ctxT": a["ctx_1024"].transpose(0, 2, 1), "g_x": a["g_xattn"], "g_f": a["g_ffn"],
        "inT": a["L0_xattn_in_proj_w"].T, "convw": a["L0_xattn_conv_w"], "convb": a["L0_xattn_conv_b"],
        "xpT": xpT, "dtwT": a["L0_xattn_dt_proj_w"].T, "dtb": a["L0_xattn_dt_proj_b"],
        "alog": a["L0_xattn_A_log"], "dvec": a["L0_xattn_D"], "gateT": a["L0_ffn_gate_w"].T, "wall": wall,
        "ident_d": np.eye(P, dtype=np.float32), "iota_d": np.tile(np.arange(DS, dtype=np.float32), (P, 1)),
        "tri_d": np.triu(np.ones((P, P), np.float32), 1), "ones_d": np.ones((P, P), np.float32), "reset_d": reset,
        "steps_d": np.tile(np.arange(TT, dtype=np.float32) * P, (P, 1)), "tile_d": np.tile(number, (P, 1, 1)),
        "ids_d": np.int32(P) * (np.arange(NS, dtype=np.int32) % TT) + part, "trash_d": TOKENS + part + np.zeros((P, NR), np.int32),
    }
    arrays = {f"in_{k}": np.ascontiguousarray(v) for k, v in arrays.items()}
    nc = bacc.Bacc("TRN2", target_bir_lowering=False, num_devices=1)
    args = [nc.dram_tensor(k, v.shape, mybir.dt.from_np(v.dtype), kind="ExternalInput").ap() for k, v in arrays.items()]
    out = nc.dram_tensor("out_x", (NB, L, H), F32, kind="ExternalOutput").ap()
    mamba_moe(nc, *args, out)
    r = run_bass_kernel_spmd(nc, [arrays], core_ids=[0])
    return r.results[0]["out_x"]
```

```python
from contextlib import ExitStack

import concourse.bass as bass
from concourse import mybir

F32 = mybir.dt.float32
F32R = mybir.dt.float32r
I32 = mybir.dt.int32
U32 = mybir.dt.uint32
ALU = mybir.AluOpType
ACT = mybir.ActivationFunctionType
AX = mybir.AxisListType

P = 128
NB, L, H = 4, 512, 512
DM, DI, DS, DR, DC = 256, 512, 16, 16, 4
J = DI // P
TC = L // P
KC = DM // P
E, TOPK, I = 16, 6, 352
NX = E + 2
HK = H // P
IP = 384
IK = IP // P
WCOLS = HK * 2 * I + IK * H
W2AT = HK * 2 * I
ROW = H + NX + 2
TOKENS = NB * L
TT = TOKENS // P
NS = 2 * TT
NR = TOPK * TT + E
NT = NS + NR
LISTS = TT * TOPK // 4
SHARE = WCOLS // 2
PEELED = 7
AHEAD = 5
DTP, BP, CP, XP = 0, 32, 64, 80
LN_EPS = 1e-5

PE_WORK = {0: [("inproj", "pre", 0)], 1: [("inproj", "pre", 1)],
           2: [("inproj", "pre", 2), ("yt", "epi", 0)], 3: [("inproj", "pre", 3), ("yt", "epi", 1)],
           4: [("yt", "epi", 2), ("yt", "epi", 3)], 7: [("xproj", "pre", 0), ("xlt", "epi", 0)],
           8: [("dt", "pre", 0), ("dt", "pre", 1)], 9: [("dt", "pre", 2), ("dt", "pre", 3)],
           10: [("bt", "pre", 0), ("xlt", "epi", 1)], 11: [("xlt", "epi", 2), ("xlt", "epi", 3)],
           12: [("dut", "pre", 0), ("gate", "epi", 0)], 13: [("dut", "pre", 1)], 14: [("dut", "pre", 2)],
           15: [("dut", "pre", 3)]}
ACT_WORK = {1: [("inproj", "pre", 0)], 2: [("inproj", "pre", 1)], 3: [("inproj", "pre", 2)], 4: [("inproj", "pre", 3)],
            6: [("rstd", "both", 0)], 7: [("silu", "pre", 0), ("siluz", "own", 0)],
            8: [("xproj", "pre", 0), ("xlt", "epi", 0)], 10: [("softplus", "pre", 0)],
            11: [("bt", "pre", 0), ("xlt", "epi", 1)], 12: [("xlt", "epi", 2), ("xlt", "epi", 3)],
            13: [("dut", "pre", 0), ("gate", "epi", 0)], 14: [("dut", "pre", 1)], 15: [("dut", "pre", 2), ("dut", "pre", 3)]}
DVE_WORK = {0: [("y", "epi", 0)], 1: [("inproj", "pre", 0), ("yz", "epi", 0)], 2: [("inproj", "pre", 1), ("yt", "epi", 0)],
            3: [("inproj", "pre", 2), ("yt", "epi", 1)], 4: [("inproj", "pre", 3), ("yt", "epi", 2), ("yt", "epi", 3)],
            5: [("stats2", "epi", 0), ("stats", "own", 0)], 6: [("nmr", "own", 0), ("norm", "epi", 0)],
            8: [("dt", "pre", 0), ("dt", "pre", 1)], 9: [("dt", "pre", 2), ("dt", "pre", 3)],
            11: [("delta", "pre", 0)], 12: [("gate", "epi", 0), ("delta", "pre", 1)], 13: [("delta", "pre", 2)],
            14: [("delta", "pre", 3)], 15: [("gate", "epi", 1)]}
SP_WORK = {0: [("load", "pre", 0)], 5: [("norm", "epi", 0)], 8: [("xproj", "pre", 0), ("xrow", "pre", 0)],
           15: [("gate", "epi", 0)]}
BANK_USES = [(kind, i) for n in sorted(PE_WORK) for kind, whose, i in PE_WORK[n]]
USES = tuple(len(BANK_USES[k::2]) for k in range(2))


def use(kind, i, q):
    at = BANK_USES.index((kind, i))
    late = 2 if kind in ("yt", "xlt", "gate") else 0
    return at % 2, (q + late) * USES[at % 2] + at // 2


def batch_steps(work, b):
    first, last = isinstance(b, int) and b < 1, isinstance(b, int) and b >= NB - 1
    scanned = not isinstance(b, int) or 0 <= b < NB
    out = []
    for n in range(DS):
        if scanned:
            out.append(("step", b, n))
        for kind, whose, i in work.get(n, ()):
            if whose == "pre":
                out.append(("skip" if last else kind, b + 1, (kind, i) if last else i))
            elif whose == "epi":
                out.append(("skip" if first else kind, b - 1, (kind, i) if first else i))
            elif scanned or (whose == "both" and not (isinstance(b, int) and b < 0)):
                out.append((kind, b, i))
        if scanned:
            out.append(("rest", b, n))
    return out


def stage_a(eng, work, handlers, between=None, after_scans=None):
    def run(b):
        for kind, q, i in batch_steps(work, b):
            if kind in handlers:
                handlers[kind](q, i)

    run(-1)
    if between:
        between()
    run(0)
    with eng.Fori(1, NB - 1) as b:
        run(b)
    run(NB - 1)
    if after_scans:
        after_scans()
    run(NB)


def mamba_moe(nc, x, ctxT, g_x, g_f, inT, convw, convb, xpT, dtwT, dtb, alog, dvec,
              gateT, wall, ident_d, iota_d, tri_d, ones_d, reset_d, steps_d, tile_d, ids_d, trash_d, out):
    rows_d = nc.dram_tensor("token_rows", (TOKENS + P, ROW), F32, kind="Internal").ap()
    acc_d = nc.dram_tensor("sums", (TOKENS + P, H), F32, kind="Internal").ap()
    list_d = nc.dram_tensor("token_lists", (P * NR, 1), I32, kind="Internal").ap()
    c_d = nc.dram_tensor("c_rows", (NB, DS, L), F32, kind="Internal").ap()
    x_rows = x.rearrange("b (c p) h -> b p c h", p=P)
    acc_v = acc_d[0:TOKENS, :].rearrange("(b c p) h -> b p c h", p=P, c=TC)
    rows_v = rows_d[0:TOKENS, :].rearrange("(b c p) h -> b p c h", p=P, c=TC)

    with ExitStack() as ctx:
        def alloc(stack, name, shape, dt=F32):
            return stack.enter_context(nc.sbuf_tensor(name, shape, dt))

        def sem(name):
            return ctx.enter_context(nc.semaphore(name))

        banks = [ctx.enter_context(nc.psum_tensor(f"bank{i}", [P, 512], F32)) for i in range(8)]
        ysum, dbu, misc = banks[0:4], banks[4:6], banks[6:8]

        ident = alloc(ctx, "ident", [P, P])
        zero = alloc(ctx, "zero", [P, ROW])
        sel = alloc(ctx, "sel", [P, E, TT])
        ids = alloc(ctx, "ids", [P, NT], I32)
        own = alloc(ctx, "own", [P, TT], I32)
        tri = alloc(ctx, "tri", [P, P])
        ones = alloc(ctx, "ones", [P, P])
        reset = alloc(ctx, "reset", [P, E, TT])
        steps = alloc(ctx, "steps", [P, TT])
        tileno = alloc(ctx, "tileno", [P, 2, NT])
        iotab = alloc(ctx, "iotab", [P, E])
        xt = alloc(ctx, "xt", [P, 4, ROW])
        choice = alloc(ctx, "choice", [P, TT, TOPK])

        mem = ExitStack()
        gt = alloc(mem, "gt", [P, 2, TC, DI])
        dA = alloc(mem, "dA", [P, 4, L])
        hs = alloc(mem, "hs", [P, 4, L])
        crow = alloc(mem, "crow", [P, 4, L])
        hc = alloc(mem, "hc", [P, 4, L])
        delta = alloc(mem, "delta", [P, 2, J, L])
        duT = alloc(mem, "duT", [P, 2, TC, DI])
        sw = alloc(mem, "sw", [P, J, L])
        st1 = alloc(mem, "st1", [P, L])
        st2 = alloc(mem, "st2", [P, L])
        ctxt = alloc(mem, "ctxt", [P, KC, L])
        xpad = alloc(mem, "xpad", [P, J, L + 4])
        xd = alloc(mem, "xd", [XP, L])
        iota16 = alloc(mem, "iota16", [P, DS])
        inw = alloc(mem, "inw", [P, KC, DI])
        xpw = alloc(mem, "xpw", [P, J, XP])
        dtw = alloc(mem, "dtw", [DR, DI])
        cw = alloc(mem, "cw", [P, J, DC])
        cb = alloc(mem, "cb", [P, J])
        dtbias = alloc(mem, "dtbias", [P, J])
        dsk = alloc(mem, "dsk", [P, J])
        aneg = alloc(mem, "aneg", [P, J, DS])
        aexp = alloc(mem, "aexp", [P, J, DS])
        gx = alloc(mem, "gx", [P, 1])
        gf = alloc(mem, "gf", [P, 1])
        tgx = alloc(mem, "tgx", [P, 1])
        tgf = alloc(mem, "tgf", [P, 1])
        gw = alloc(mem, "gw", [P, HK, E])
        eps = alloc(mem, "eps", [P, 1])
        one = alloc(mem, "one", [P, 1])
        xrow = alloc(mem, "xrow", [P, 2, TC, H])
        u = alloc(mem, "u", [P, 2, J, L])
        sz = alloc(mem, "sz", [P, J, L])
        bst = alloc(mem, "bst", [P, TC, 6])
        bag = alloc(mem, "bag", [P, TC, 2])
        lnv = alloc(mem, "lnv", [P, TC])
        lnv2 = alloc(mem, "lnv2", [P, TC])
        rstd = alloc(mem, "rstd", [P, TC])
        nmr = alloc(mem, "nmr", [P, TC])
        du = alloc(mem, "du", [P, J, L])
        y = du
        btn = alloc(mem, "btn", [P, TC, DS])
        btc = alloc(mem, "btc", [P, TC, DS])
        bst2 = alloc(mem, "bst2", [P, TC, 6])
        bag2 = alloc(mem, "bag2", [P, TC, 2])
        rstd2 = alloc(mem, "rstd2", [P, TC])
        rowb = alloc(mem, "rowb", [P, TC, ROW])
        xlT = alloc(mem, "xlT", [P, TC, HK, P])
        mx = alloc(mem, "mx", [P, TC])
        lgs = alloc(mem, "lgs", [P, TC, E])
        ex = alloc(mem, "ex", [P, TC, E])
        sm = alloc(mem, "sm", [P, TC])
        rsm = alloc(mem, "rsm", [P, TC])
        sc = alloc(mem, "sc", [P, TC, E])
        m8 = alloc(mem, "m8", [P, TC, 8])
        ix = alloc(mem, "ix", [P, TC, 8], U32)
        ixf = alloc(mem, "ixf", [P, TC, 8])
        eq = alloc(mem, "eq", [P, TC, E, TOPK])
        mask = alloc(mem, "mask", [P, TC, E])
        s6 = alloc(mem, "s6", [P, TC])
        r6 = alloc(mem, "r6", [P, TC])
        r6g = alloc(mem, "r6g", [P, TC])
        mem.close()

        wraw = alloc(ctx, "wraw", [P, WCOLS])
        wh = alloc(ctx, "wh", [P, 2 * WCOLS], F32R)
        wl = alloc(ctx, "wl", [P, 2 * WCOLS], F32R)
        xh = alloc(ctx, "xh", [P, 2, H], F32R)
        xl = alloc(ctx, "xl", [P, 2, H], F32R)
        cc = alloc(ctx, "cc", [P, 2])
        sg = alloc(ctx, "sg", [P, 2, I])
        am = alloc(ctx, "am", [P, 2, IP])
        ah = alloc(ctx, "ah", [P, 2, IP], F32R)
        al = alloc(ctx, "al", [P, 2, IP], F32R)
        ys = alloc(ctx, "ys", [P, 4, H])
        meta = alloc(ctx, "meta", [P, 3, NT], I32)
        gid = alloc(ctx, "gid", [P, 4], I32)
        aid = alloc(ctx, "aid", [P, 4], I32)
        total = alloc(ctx, "total", [P, E, TT])
        before = alloc(ctx, "before", [P, E, TT])
        upto = alloc(ctx, "upto", [P, E, TT])
        over = alloc(ctx, "over", [P, E, TT])
        tiles_e = alloc(ctx, "tiles_e", [P, E])
        one_e = alloc(ctx, "one_e", [P, E])
        end_e = alloc(ctx, "end_e", [P, E])
        first_e = alloc(ctx, "first_e", [P, E])
        rank = alloc(ctx, "rank", [P, E, TT])
        ranki = alloc(ctx, "ranki", [P, E, TT], I32)
        lowi = alloc(ctx, "lowi", [P, E, TT], I32)
        highi = alloc(ctx, "highi", [P, E, TT], I32)
        place = alloc(ctx, "place", [P, E, TT])
        eqb = alloc(ctx, "eqb", [P, TT, TOPK, E])
        posf = alloc(ctx, "posf", [P, TT, TOPK])
        posi = alloc(ctx, "posi", [P, TT * TOPK], I32)
        cur = alloc(ctx, "cur", [P, 4], I32)
        past = alloc(ctx, "past", [P, NT, E - 1])
        slot = alloc(ctx, "slot", [P, NT])
        sloti = alloc(ctx, "sloti", [P, NT], I32)
        odd = alloc(ctx, "odd", [P, NT], I32)
        fresh = alloc(ctx, "fresh", [P, NT])
        lasti = alloc(ctx, "lasti", [P, 1], I32)
        fours = alloc(ctx, "fours", [P, 2], I32)

        const_in = sem("const_in")
        setup_act = sem("setup_act")
        setup_dve = sem("setup_dve")
        ctx_in = sem("ctx_in")
        xrow_in = sem("xrow_in")
        full = [sem("misc_full0"), sem("misc_full1")]
        gone = [sem("misc_gone0"), sem("misc_gone1")]
        stats_done = sem("stats_done")
        lnv_done = sem("lnv_done")
        lnv2_done = sem("lnv2_done")
        rstd_done = sem("rstd_done")
        nmr_done = sem("nmr_done")
        bst_done = sem("bst_done")
        conv_done = sem("conv_done")
        silu_done = sem("silu_done")
        siluz_done = sem("siluz_done")
        cd_stored = sem("cd_stored")
        crow_in = [sem(f"crow_in{i}") for i in range(4)]
        nv_done = sem("nv_done")
        se_done = sem("se_done")
        sw_done = sem("sw_done")
        st_done = sem("st_done")
        delta_done = sem("delta_done")
        du_done = sem("du_done")
        btc_done = sem("btc_done")
        g_done = sem("g_done")
        turned = sem("turned")
        dA_done = sem("dA_done")
        scanned = sem("scanned")
        hc_done = sem("hc_done")
        summed = sem("summed")
        y_done = sem("y_done")
        yz_done = sem("yz_done")
        x2_done = sem("x2_done")
        bag2_done = sem("bag2_done")
        rstd2_done = sem("rstd2_done")
        norm_done = sem("norm_done")
        base_stored = sem("base_stored")
        rows_stored = sem("rows_stored")
        gate_step = sem("gate_step")
        exp_done = sem("exp_done")
        raw_in = sem("raw_in")
        wh_done = sem("wh_done")
        wl_done = sem("wl_done")
        gathered = sem("gathered")
        zero_done = sem("zero_done")
        blank_in = sem("blank_in")
        plan_in = sem("plan_in")
        sel_done = sem("sel_done")
        counted = sem("counted")
        plan_step = sem("plan_step")
        meta_ready = sem("meta_ready")
        counts_read = sem("counts_read")
        pos_ready = sem("pos_ready")
        listed = sem("listed")
        cur_done = sem("cur_done")
        gid_done = sem("gid_done")
        aid_done = sem("aid_done")
        ids_in = sem("ids_in")
        copied = sem("copied")
        xt_turned = sem("xt_turned")
        xh_done = sem("xh_done")
        xl_done = sem("xl_done")
        cc_done = sem("cc_done")
        up_done = sem("up_done")
        sg_done = sem("sg_done")
        am_done = sem("am_done")
        am_turned = sem("am_turned")
        ah_done = sem("ah_done")
        al_done = sem("al_done")
        down_done = sem("down_done")
        ys_done = sem("ys_done")
        added = sem("added")
        pad_done = sem("pad_done")

        GATE_STEPS = 15
        N_CONST = 13
        N_PLAN = 8
        PLAN_STEPS = 22

        def at_least(eng, s, v):
            if isinstance(v, int) and v <= 0:
                return
            eng.wait_ge(s, v)

        waited = {e: sem(f"waited_{e}") for e in ("sp", "act", "dve", "pe", "pool")}

        def apart(eng, s, v, who):
            at_least(eng, s, v)
            if not isinstance(v, int):
                eng.sem_inc(waited[who], 1)

        def tile_groups(eng):
            return eng.value_load(fours[0:1, 0:1], min_val=(NS + E) // 4, max_val=NT // 4)

        def tiles_but_12(eng):
            return eng.value_load(fours[0:1, 1:2], min_val=NS + E - 12, max_val=NT - 12)

        block = ctx.enter_context(nc.Block())

        @block.sync
        def _(sp):
            consts = [(ident, ident_d), (iota16, iota_d), (inw, inT.rearrange("(k p) e -> p k e", p=P)),
                      (xpw, xpT.rearrange("(k p) m -> p k m", p=P)), (dtw, dtwT),
                      (cw, convw.rearrange("(j p) c -> p j c", p=P)), (cb, convb.rearrange("(j p) -> p j", p=P)),
                      (dtbias, dtb.rearrange("(j p) -> p j", p=P)), (dsk, dvec.rearrange("(j p) -> p j", p=P)),
                      (aexp, alog.rearrange("(j p) n -> p j n", p=P)), (gw, gateT.rearrange("(k p) e -> p k e", p=P)),
                      (gx, g_x.partition_broadcast(P)), (gf, g_f.partition_broadcast(P))]
            with nc.allow_non_contiguous_dma(reason="per-channel vectors of 512 values"):
                for dst, src in consts:
                    sp.dma_start(dst[:], src).then_inc(const_in, 16)
                sp.wait_ge(zero_done, 1)
                sp.dma_start(rows_d[TOKENS:TOKENS + P, :], zero[:]).then_inc(rows_stored, 16)
                sp.dma_start(acc_d[TOKENS:TOKENS + P, :], zero[:, 0:H]).then_inc(base_stored, 16)
                sp.dma_start(list_d.rearrange("(p t) a -> p (t a)", p=P), trash_d).then_inc(blank_in, 16)

            def load(q, _):
                if not (isinstance(q, int) and q == 0):
                    bank, m = use("inproj", 3, q - 1)
                    apart(sp, full[bank], m + 1, "sp")
                sp.dma_start(ctxt[:], ctxT[bass.ds(q, 1)].rearrange("a (k p) t -> p (a k) t", p=P)).then_inc(ctx_in, 16)

            def xrow_(q, _):
                if not (isinstance(q, int) and q < 2):
                    apart(sp, base_stored, 16 * q, "sp")
                    apart(sp, norm_done, TC * (q - 1), "sp")
                sp.dma_start(xrow[:, bass.ds(q % 2, 1)].rearrange("p a c h -> p (a c) h"),
                             x_rows[bass.ds(q, 1)].rearrange("a p c h -> p (a c) h")).then_inc(xrow_in, 16)

            def xproj(q, _):
                bank, m = use("xproj", 0, q)
                apart(sp, gone[bank], m + 1, "sp")
                sp.dma_start(c_d[bass.ds(q, 1)].rearrange("a n t -> (a n) t"), xd[CP:CP + DS, :]).then_inc(cd_stored, 16)

            def c_row(b, n):
                if n == 0:
                    apart(sp, cd_stored, 16 * (b + 1), "sp")
                apart(sp, hc_done, (b * DS + n - 3) * J, "sp")
                src = c_d[bass.ds(b, 1), n, :].rearrange("a t -> (a t)")
                sp.dma_start(crow[:, n % 4, :], src.partition_broadcast(P)).then_inc(crow_in[n % 4], 16)

            def step(b, n):
                if n + 3 < DS:
                    c_row(b, n + 3)
                elif not (isinstance(b, int) and b == NB - 1):
                    c_row(b + 1, n + 3 - DS)

            def norm(b, _):
                apart(sp, x2_done, TC * (b + 1), "sp")
                sp.dma_start(acc_v[bass.ds(b, 1)].rearrange("a p c h -> p (a c) h"), xrow[:, bass.ds(b % 2, 1)].rearrange("p a c h -> p (a c) h")).then_inc(base_stored, 16)

            def gate(b, _):
                apart(sp, gate_step, GATE_STEPS * (b + 1), "sp")
                apart(sp, norm_done, TC * (b + 1), "sp")
                sp.dma_start(rows_v[bass.ds(b, 1)].rearrange("a p c h -> p (a c) h"), rowb[:]).then_inc(rows_stored, 16)

            def first_rows():
                for n in range(3):
                    c_row(0, n)
                for dst, src in ((ids[:, 0:NS], ids_d), (own[:], ids_d[:, 0:TT]), (tri[:], tri_d), (ones[:], ones_d),
                                 (reset[:], reset_d), (steps[:], steps_d), (tileno[:], tile_d), (iotab[:], iota_d)):
                    sp.dma_start(dst, src).then_inc(plan_in, 16)

            def fetch(e):
                at_least(sp, wl_done, e)
                sp.dma_start(wraw[:], wall[bass.ds(e, 1)].rearrange("a p c -> p (a c)")).then_inc(raw_in, 16)

            def first_weights():
                sp.wait_ge(summed, NB * DS * J)
                fetch(0)

            stage_a(sp, SP_WORK, {"load": load, "xrow": xrow_, "xproj": xproj, "step": step, "norm": norm, "gate": gate},
                    first_rows, first_weights)

            sp.wait_ge(rows_stored, 16 * (NB + 1))
            sp.wait_ge(base_stored, 16 * (NB + 1))
            sp.wait_ge(norm_done, TC * NB)

            fetch(1)
            fetch(2)
            sp.wait_ge(listed, 16 * TOPK * TT)
            sp.dma_start(ids[:, NS:NT], list_d.rearrange("(p t) a -> p (t a)", p=P)).then_inc(ids_in, 16)
            with sp.Fori(3, NX) as e:
                fetch(e)
            apart(sp, added, 16 * (tiles_but_12(sp) + 12), "sp")
            sp.dma_start(out.rearrange("b s h -> (b s) h"), acc_d[0:TOKENS, :]).then_inc(copied, 16)
            sp.wait_ge(copied, 16)

        @block.scalar
        def _(act):
            act.wait_ge(const_in, 16 * N_CONST)
            nc.scalar.activation(aneg[:], aexp[:], ACT.Exp).then_inc(setup_act, 1)
            nc.scalar.activation(tgx[:], gx[:], ACT.Tanh).then_inc(setup_act, 1)
            nc.scalar.activation(tgf[:], gf[:], ACT.Tanh).then_inc(setup_act, 1)
            act.wait_ge(setup_dve, 1)

            def evacuate(stage, i, q, dst, cols, parts=P):
                bank, m = use(stage, i, q)
                apart(act, full[bank], m + 1, "act")
                nc.scalar.copy(dst, misc[bank][0:parts, 0:cols]).then_inc(gone[bank], 1)

            def rstd_(b, _):
                own = not (isinstance(b, int) and b == NB)
                before = not (isinstance(b, int) and b == 0)
                if own:
                    apart(act, stats_done, b + 1, "act")
                    nc.scalar.activation(lnv[:], bag[:, :, 1], ACT.Ln, bias=eps[:]).then_inc(lnv_done, 1)
                if before:
                    apart(act, bag2_done, b, "act")
                    nc.scalar.activation(lnv2[:], bag2[:, :, 1], ACT.Ln, bias=eps[:]).then_inc(lnv2_done, 1)
                if own:
                    apart(act, lnv_done, b + 1, "act")
                    nc.scalar.activation(rstd[:], lnv[:], ACT.Exp, scale=-0.5).then_inc(rstd_done, 1)
                if before:
                    apart(act, lnv2_done, b, "act")
                    nc.scalar.activation(rstd2[:], lnv2[:], ACT.Exp, scale=-0.5).then_inc(rstd2_done, 1)

            def inproj(q, j):
                at_least(act, conv_done, DC * (J * (q - 1) + j + 1) if not (isinstance(q, int) and q == 0) else 0)
                evacuate("inproj", j, q, xpad[:, j, 3:3 + L], L)

            def silu(q, _):
                for j in range(J):
                    apart(act, conv_done, DC * (J * q + j + 1), "act")
                    uj = u[:, bass.ds(q % 2, 1), j, :].rearrange("p a t -> p (a t)")
                    nc.scalar.activation(uj, uj, ACT.Silu, bias=cb[:, j:j + 1]).then_inc(silu_done, 1)

            def siluz(b, _):
                apart(act, nmr_done, b + 1, "act")
                apart(act, yz_done, J * b, "act")
                for j in range(J):
                    nc.scalar.activation(sz[:, j, :], xrow[:, bass.ds(b % 2, 1), j, :].rearrange("p a t -> p (a t)"),
                                         ACT.Silu, bias=nmr[:, j:j + 1], scale=rstd[:, j:j + 1]).then_inc(siluz_done, 1)

            def xproj(q, _):
                at_least(act, cd_stored, 16 * q)
                if not (isinstance(q, int) and q == 0):
                    bank, m = use("bt", 0, q - 1)
                    act.wait_ge(full[bank], m + 1)
                evacuate("xproj", 0, q, xd[:], L, XP)

            def bt(q, _):
                evacuate("bt", 0, q, btn[:].rearrange("p c n -> p (c n)"), TC * DS)

            def softplus(q, _):
                for j in range(J):
                    apart(act, nv_done, J * q + j + 1, "act")
                    nc.scalar.activation(du[:, j, :], du[:, j, :], ACT.Exp).then_inc(se_done, 1)
                at_least(act, st_done, 3 * J * q)
                for j in range(J):
                    apart(act, se_done, J * q + j + 1, "act")
                    nc.scalar.activation(sw[:, j, :], du[:, j, :], ACT.Ln, bias=one[:]).then_inc(sw_done, 1)

            def dut(q, j):
                bank, m = use("dut", j, q)
                apart(act, full[bank], m + 1, "act")
                nc.scalar.copy(duT[:, bass.ds(q % 2, 1), :, j * P:(j + 1) * P].rearrange("p a c t -> p (a c) t"),
                               misc[bank][:].rearrange("p (c t) -> p c t", t=P)).then_inc(gone[bank], 1)

            def step(b, n):
                if n == 0:
                    bank, m = use("dut", 3, b)
                    act.wait_ge(gone[bank], m + 1)
                    at_least(act, g_done, DS * b)
                    nc.scalar.copy(btc[:], btn[:]).then_inc(btc_done, 1)
                    apart(act, btc_done, b + 1, "act")
                    bank, m = use("dut", 2, b)
                    apart(act, gone[bank], m + 1, "act")
                    apart(act, delta_done, J * (b + 1), "act")
                apart(act, turned, J * (b * DS + n - 1), "act")
                for t in range(TC):
                    g = nc.scalar.activation(gt[:, n % 2, t, :], duT[:, bass.ds(b % 2, 1), t, :].rearrange("p a t -> p (a t)"),
                                             ACT.Copy, scale=btc[:, t, n:n + 1])
                g.then_inc(g_done, 1)
                for j in range(J):
                    apart(act, scanned, (b * DS + n - 1) * J + j + 1, "act")
                    nc.scalar.activation(dA[:, j, :], delta[:, bass.ds(b % 2, 1), j, :].rearrange("p a t -> p (a t)"),
                                         ACT.Exp, scale=aneg[:, j, n:n + 1]).then_inc(dA_done, 1)

            def xlt(b, t):
                evacuate("xlt", t, b, xlT[:, t, :, :].rearrange("p k m -> p (k m)"), H)

            def gate(b, _):
                bank, m = use("gate", 0, b)
                act.wait_ge(gone[bank], m + 1)
                nc.scalar.activation(ex[:], lgs[:], ACT.Exp).then_inc(exp_done, 1)

            def split_high(e, t):
                mine = WCOLS if isinstance(e, int) else WCOLS - SHARE
                apart(act, raw_in, 16 * (e + 1), "act")
                apart(act, down_done, t, "act")
                nc.scalar.copy(wh[:, bass.ds((e % 2) * WCOLS, mine)], wraw[:, 0:mine]).then_inc(wh_done, 2 if mine == WCOLS else 1)

            def first_weights():
                act.wait_ge(summed, NB * DS * J)
                split_high(0, 0)

            act.wait_ge(setup_dve, 2)
            stage_a(act, ACT_WORK, {"rstd": rstd_, "inproj": inproj, "silu": silu, "siluz": siluz, "xproj": xproj, "bt": bt,
                                    "softplus": softplus, "dut": dut, "step": step, "xlt": xlt, "gate": gate},
                    after_scans=first_weights)

            def x_high(t, s):
                act.wait_ge(xt_turned, t + 1)
                at_least(act, up_done, t - 1)
                nc.scalar.copy(xh[:, s, :], banks[0][:]).then_inc(xh_done, 1)

            def gate_up(t, s):
                act.wait_ge(up_done, t + 1)
                at_least(act, am_done, t - 1)
                nc.scalar.activation(sg[:, s, :], banks[1 + 2 * s][:, 0:I], ACT.Silu).then_inc(sg_done, 1)

            def a_high(t, s):
                act.wait_ge(am_turned, t + 1)
                at_least(act, down_done, t - 1)
                nc.scalar.copy(ah[:, s, :], banks[5][:, 0:IP]).then_inc(ah_done, 1)

            def y_out(t, s, slot):
                apart(act, down_done, t + 1, "act")
                apart(act, added, 16 * (t - 3), "act")
                nc.scalar.copy(ys[:, bass.ds(slot, 1), :].rearrange("p a h -> p (a h)"), banks[6 + s][:]).then_inc(ys_done, 1)

            def next_weights(t):
                e = act.value_load(meta[0:1, 2, bass.ds(t, 1)], min_val=0, max_val=NX - 1)
                with act.If(e > 0):
                    split_high(e, t)

            act.wait_ge(rows_stored, 16 * (NB + 1))
            act.wait_ge(base_stored, 16 * (NB + 1))
            x_high(0, 0)
            x_high(1, 1)
            split_high(1, 0)
            gate_up(0, 0)
            for t in range(1, PEELED):
                a_high(t - 1, (t - 1) % 2)
                x_high(t + 1, (t + 1) % 2)
                gate_up(t, t % 2)
                y_out(t - 1, (t - 1) % 2, (t - 1) % 4)
            act.wait_ge(meta_ready, 1)
            groups = tile_groups(act)
            with act.Fori(PEELED // 2, 2 * groups - 1) as i:
                for k in (1, 2):
                    t, s = 2 * i + k, k % 2
                    a_high(t - 1, 1 - s)
                    x_high(t + 1, 1 - s)
                    gate_up(t, s)
                    y_out(t - 1, 1 - s, (t - 1) % 4)
                    next_weights(t)
            last = tiles_but_12(act) + 11
            a_high(last - 1, 0)
            gate_up(last, 1)
            y_out(last - 1, 0, 2)
            next_weights(last)
            a_high(last, 1)
            y_out(last, 1, 3)

        @block.gpsimd
        def _(pool):
            def step(b, n):
                pool.wait_ge(crow_in[n % 4], 16 * (b * (DS // 4) + n // 4 + 1))
                for j in range(J):
                    i = (b * DS + n) * J + j
                    pool.wait_ge(scanned, i + 1)
                    at_least(pool, summed, i - 3)
                    nc.gpsimd.tensor_tensor(hc[:, j, :], hs[:, j, :], crow[:, n % 4, :], ALU.mult).then_inc(hc_done, 1)

            stage_a(pool, {}, {"step": step})

            def split_low(e):
                half = bass.ds((e % 2) * WCOLS, WCOLS)
                apart(pool, wh_done, 2 * (e + 1), "pool")
                nc.gpsimd.tensor_tensor(wl[:, half], wraw[:], wh[:, half], ALU.subtract).then_inc(wl_done, 1)

            def gather(t, s, rows=TOKENS + P):
                apart(pool, xt_turned, t - 3, "pool")
                apart(pool, cc_done, t - 3, "pool")
                apart(pool, gathered, 16 * t, "pool")
                nc.gpsimd.tensor_copy(gid[:, s:s + 1], ids[:, bass.ds(t, 1)]).then_inc(gid_done, 1)
                apart(pool, gid_done, t + 1, "pool")
                pool.indirect_dma_start(xt[:, s, :], None, rows_d[0:rows, :], bass.IndirectOffsetOnAxis(ap=gid[:, s:s + 1], axis=0)).then_inc(gathered, 16)

            def add(t, s):
                apart(pool, ys_done, t + 1, "pool")
                apart(pool, added, 16 * t, "pool")
                nc.gpsimd.tensor_copy(aid[:, s:s + 1], ids[:, bass.ds(t, 1)]).then_inc(aid_done, 1)
                apart(pool, aid_done, t + 1, "pool")
                pool.indirect_dma_start(acc_d[:, :], bass.IndirectOffsetOnAxis(ap=aid[:, s:s + 1], axis=0), ys[:, s, :], None,
                                        compute_op=ALU.add).then_inc(added, 16)

            def list_tokens(i, k):
                apart(pool, listed, 16 * 4 * i, "pool")
                nc.gpsimd.tensor_copy(cur[:], posi[:, bass.ds(i * 4, 4)]).then_inc(cur_done, 1)
                apart(pool, cur_done, i + 1, "pool")
                for c in range(4):
                    pool.indirect_dma_start(list_d[:, :], bass.IndirectOffsetOnAxis(ap=cur[:, c:c + 1], axis=0),
                                            own[:, 4 * k + c:4 * k + c + 1], None).then_inc(listed, 16)

            def next_weights(t):
                e = pool.value_load(meta[0:1, 2, bass.ds(t, 1)], min_val=0, max_val=NX - 1)
                with pool.If(e > 0):
                    split_low(e)

            pool.wait_ge(summed, NB * DS * J)
            pool.wait_ge(plan_in, 16 * N_PLAN)
            pool.wait_ge(rows_stored, 16 * NB)
            for t in range(4):
                gather(t, t, (NB - 1) * L)
            split_low(0)
            pool.wait_ge(rows_stored, 16 * (NB + 1))
            pool.wait_ge(base_stored, 16 * (NB + 1))

            pool.wait_ge(blank_in, 16)

            gather(4, 0)
            split_low(1)
            for t in range(8):
                gather(t + AHEAD, (t + AHEAD) % 4)
                add(t, t % 4)
                if t == 0:
                    pool.wait_ge(pos_ready, 1)
                list_tokens(t, t % 4)
            pool.wait_ge(meta_ready, 1)
            with pool.Fori(2, LISTS // 4) as i:
                for k in range(4):
                    gather(4 * i + k + AHEAD, (k + AHEAD) % 4)
                    next_weights(4 * i + k)
                    add(4 * i + k, k)
                    list_tokens(4 * i + k, k)
            for t in range(LISTS, LISTS + 4):
                if t + AHEAD == NS:
                    pool.wait_ge(ids_in, 16)
                gather(t + AHEAD, (t + AHEAD) % 4)
                next_weights(t)
                add(t, t % 4)
            groups = tile_groups(pool)
            with pool.Fori(LISTS // 4 + 1, groups - 2) as i:
                for k in range(4):
                    gather(4 * i + k + AHEAD, (k + AHEAD) % 4)
                    next_weights(4 * i + k)
                    add(4 * i + k, k)
            rest = tiles_but_12(pool) + 4
            for k in range(8):
                if k + AHEAD < 8:
                    gather(rest + k + AHEAD, (k + AHEAD) % 4)
                next_weights(rest + k)
                add(rest + k, k % 4)

        @block.vector
        def _(dve):
            nc.vector.memset(eps[:], LN_EPS)
            nc.vector.memset(one[:], 1.0)
            nc.vector.memset(xpad[:], 0.0).then_inc(setup_dve, 1)
            dve.wait_ge(setup_act, 3)
            nc.vector.tensor_scalar(aneg[:], aneg[:], -1.0, None, ALU.mult).then_inc(setup_dve, 1)
            nc.vector.memset(zero[:], 0.0).then_inc(zero_done, 1)
            nc.vector.memset(rowb[:], 1.0).then_inc(setup_dve, 1)
            dve.wait_ge(setup_dve, 3)
            nc.vector.tensor_scalar(rowb[:, :, H:H + 2], rowb[:, :, H:H + 2], tgf[:, 0:1], None,
                                    ALU.mult).then_inc(setup_dve, 1)

            def stats(q, _):
                apart(dve, xrow_in, 16 * (q + 1), "dve")
                if not (isinstance(q, int) and q == 0):
                    apart(dve, siluz_done, J * q, "dve")
                for c in range(TC):
                    nc.vector.bn_stats(bst[:, c, :], xrow[:, bass.ds(q % 2, 1), c, :].rearrange("p a h -> p (a h)")).then_inc(bst_done, 1)
                apart(dve, bst_done, TC * (q + 1), "dve")
                for c in range(TC):
                    ins = nc.vector.bn_aggr(bag[:, c, :], bst[:, c, :])
                ins.then_inc(stats_done, 1)

            def nmr_(q, _):
                dve.wait_ge(rstd_done, q + 1)
                nc.vector.scalar_tensor_tensor(out=nmr[:], in0=bag[:, :, 0], scalar=-1.0, in1=rstd[:],
                                               op0=ALU.mult, op1=ALU.mult).then_inc(nmr_done, 1)

            def inproj(q, j):
                bank, m = use("inproj", j, q)
                dve.wait_ge(gone[bank], m + 1)
                if j == 0:
                    at_least(dve, y_done, J * (q - 1))
                uj = u[:, bass.ds(q % 2, 1), j, :].rearrange("p a t -> p (a t)")
                nc.vector.tensor_scalar(uj, xpad[:, j, 3:3 + L], cw[:, j, 3:4], None, ALU.mult).then_inc(conv_done, 1)
                for k in (2, 1, 0):
                    dve.wait_ge(conv_done, DC * (J * q + j) + 3 - k)
                    nc.vector.scalar_tensor_tensor(out=uj, in0=xpad[:, j, k:k + L], scalar=cw[:, j, k:k + 1], in1=uj,
                                                   op0=ALU.mult, op1=ALU.add).then_inc(conv_done, 1)

            def row(a, q, j):
                return a[:, bass.ds(q % 2, 1), j, :].rearrange("p a t -> p (a t)")

            def dt(q, j):
                bank, m = use("dt", j, q)
                if j == 0:
                    if not (isinstance(q, int) and q < 2):
                        apart(dve, dA_done, (q - 1) * DS * J, "dve")
                        yb, ym = use("yt", 3, q - 2)
                        apart(dve, full[yb], ym + 1, "dve")
                dve.wait_ge(full[bank], m + 1)
                nc.vector.tensor_scalar(row(delta, q, j), misc[bank][:], dtbias[:, j:j + 1], None, ALU.add).then_inc(gone[bank], 1)
                dve.wait_ge(gone[bank], m + 1)
                nc.vector.scalar_tensor_tensor(out=du[:, j, :], in0=row(delta, q, j), scalar=-1.0, in1=row(delta, q, j),
                                               op0=ALU.mult, op1=ALU.min).then_inc(nv_done, 1)

            def delta_(q, j):
                i = J * q + j
                dve.wait_ge(sw_done, i + 1)
                nc.vector.tensor_scalar(st1[:], du[:, j, :], 1.0, -1.0, ALU.add, ALU.add).then_inc(st_done, 1)
                dve.wait_ge(st_done, 3 * i + 1)
                nc.vector.tensor_tensor(st2[:], du[:, j, :], st1[:], ALU.subtract).then_inc(st_done, 1)
                dve.wait_ge(st_done, 3 * i + 2)
                nc.vector.tensor_tensor(st1[:], sw[:, j, :], st2[:], ALU.add).then_inc(st_done, 1)
                dve.wait_ge(st_done, 3 * i + 3)
                nc.vector.scalar_tensor_tensor(out=row(delta, q, j), in0=row(delta, q, j), scalar=0.0, in1=st1[:],
                                               op0=ALU.max, op1=ALU.add).then_inc(delta_done, 1)
                apart(dve, delta_done, i + 1, "dve")
                apart(dve, silu_done, J * q + j + 1, "dve")
                nc.vector.tensor_tensor(du[:, j, :], row(delta, q, j), row(u, q, j), ALU.mult).then_inc(du_done, 1)

            def step(b, n):
                for j in range(J):
                    i = (b * DS + n) * J + j
                    dve.wait_ge(dA_done, i + 1)
                    dve.wait_ge(turned, i + 1)
                    at_least(dve, hc_done, i - 3)
                    nc.vector.tensor_tensor_scan(hs[:, j, :], dA[:, j, :], dbu[j % 2][:], 0.0,
                                                 ALU.mult, ALU.add).then_inc(scanned, 1)

            def y_(b, _):
                if isinstance(b, int) and b == NB - 1:
                    bank, m = use("yt", 3, b - 1)
                else:
                    bank, m = use("dut", 3, b + 1)
                dve.wait_ge(full[bank], m + 1)
                for j in range(J):
                    dve.wait_ge(summed, ((b + 1) * DS - 1) * J + j + 1)
                    nc.vector.scalar_tensor_tensor(out=y[:, j, :], in0=row(u, b, j), scalar=dsk[:, j:j + 1], in1=ysum[j][:],
                                                   op0=ALU.mult, op1=ALU.add).then_inc(y_done, 1)

            def yz(b, _):
                for j in range(J):
                    apart(dve, y_done, J * b + j + 1, "dve")
                    dve.wait_ge(siluz_done, J * b + j + 1)
                    nc.vector.tensor_tensor(y[:, j, :], y[:, j, :], sz[:, j, :], ALU.mult).then_inc(yz_done, 1)

            def yt(b, t):
                bank, m = use("yt", t, b)
                dve.wait_ge(full[bank], m + 1)
                x2 = row(xrow, b, t)
                nc.vector.scalar_tensor_tensor(out=x2, in0=misc[bank][:], scalar=tgx[:, 0:1],
                                               in1=x2,
                                               op0=ALU.mult, op1=ALU.add).then_inc(gone[bank], 1)
                apart(dve, gone[bank], m + 1, "dve")
                nc.vector.bn_stats(bst2[:, t, :], x2).then_inc(x2_done, 1)

            def stats2(b, _):
                apart(dve, x2_done, TC * (b + 1), "dve")
                for t in range(TC):
                    ins = nc.vector.bn_aggr(bag2[:, t, :], bst2[:, t, :])
                ins.then_inc(bag2_done, 1)

            def norm(b, _):
                apart(dve, rstd2_done, b + 1, "dve")
                apart(dve, rows_stored, 16 * (b + 1), "dve")
                for t in range(TC):
                    nc.vector.tensor_scalar(rowb[:, t, 0:H], row(xrow, b, t), bag2[:, t, 0:1], rstd2[:, t:t + 1],
                                            ALU.subtract, ALU.mult).then_inc(norm_done, 1)

            def gate(b, part):
                done = [part]
                steps = GATE_STEPS * b

                def chained(ins):
                    ins.then_inc(gate_step, 1)
                    done[0] += 1
                    apart(dve, gate_step, steps + done[0], "dve")

                if part == 0:
                    bank, m = use("gate", 0, b)
                    logits = misc[bank][:, 0:TC * E].rearrange("p (c e) -> p c e", e=E)
                    dve.wait_ge(full[bank], m + 1)
                    chained(nc.vector.tensor_reduce(mx[:], logits, AX.X, ALU.max))
                    nc.vector.tensor_tensor(lgs[:], logits, mx[:].unsqueeze(2).to_broadcast([P, TC, E]),
                                            ALU.subtract).then_inc(gone[bank], 1)
                    return
                dve.wait_ge(exp_done, b + 1)
                chained(nc.vector.tensor_reduce(sm[:], ex[:], AX.X, ALU.add))
                chained(nc.vector.reciprocal(rsm[:], sm[:]))
                chained(nc.vector.tensor_tensor(sc[:], ex[:], rsm[:].unsqueeze(2).to_broadcast([P, TC, E]), ALU.mult))
                for t in range(TC):
                    ins = nc.vector.max(m8[:, t, :], sc[:, t, :])
                chained(ins)
                for t in range(TC):
                    ins = nc.vector.max_index(ix[:, t, :], m8[:, t, :], sc[:, t, :])
                chained(ins)
                chained(nc.vector.tensor_copy(ixf[:], ix[:]))
                chained(nc.vector.tensor_tensor(
                    eq[:], iota16[:].unsqueeze(1).unsqueeze(3).to_broadcast([P, TC, E, TOPK]),
                    ixf[:, :, 0:TOPK].unsqueeze(2).to_broadcast([P, TC, E, TOPK]), ALU.is_equal))
                chained(nc.vector.tensor_reduce(mask[:], eq[:], AX.X, ALU.add))
                nc.vector.tensor_copy(sel[:, :, bass.ds(b * TC, TC)].rearrange("p e c -> p c e"), mask[:]).then_inc(sel_done, 1)
                nc.vector.tensor_copy(choice[:, bass.ds(b * TC, TC), :], ixf[:, :, 0:TOPK]).then_inc(sel_done, 1)
                chained(nc.vector.tensor_tensor(sc[:], mask[:], sc[:], ALU.mult))
                chained(nc.vector.tensor_reduce(s6[:], m8[:, :, 0:TOPK], AX.X, ALU.add))
                chained(nc.vector.tensor_scalar(s6[:], s6[:], 1e-20, None, ALU.add))
                chained(nc.vector.reciprocal(r6[:], s6[:]))
                chained(nc.vector.tensor_scalar(r6g[:], r6[:], tgf[:, 0:1], None, ALU.mult))
                chained(nc.vector.tensor_tensor(rowb[:, :, H + 2:H + NX], sc[:], r6g[:].unsqueeze(2).to_broadcast([P, TC, E]), ALU.mult))
                assert done[0] == GATE_STEPS

            stage_a(dve, DVE_WORK, {"stats": stats, "inproj": inproj, "dt": dt, "delta": delta_, "step": step, "y": y_,
                                    "yz": yz, "yt": yt, "nmr": nmr_, "stats2": stats2, "norm": norm, "gate": gate})

            dve.wait_ge(rows_stored, 16 * (NB + 1))
            dve.wait_ge(base_stored, 16 * (NB + 1))
            nc.vector.memset(am[:], 0.0).then_inc(pad_done, 1)
            nc.vector.memset(one_e[:], 1.0).then_inc(pad_done, 1)
            dve.wait_ge(pad_done, 2)

            done = [0]

            def chained(ins):
                ins.then_inc(plan_step, 1)
                done[0] += 1
                dve.wait_ge(plan_step, done[0])

            def all_of(a):
                return a.rearrange("p e c -> p (e c)")

            def read_counts():
                dve.wait_ge(plan_in, 16 * N_PLAN)
                dve.wait_ge(counted, 1)
                nc.vector.tensor_copy(all_of(before[:]), banks[1][:, 0:E * TT]).then_inc(counts_read, 1)
                nc.vector.tensor_copy(all_of(total[:]), banks[0][:, 0:E * TT]).then_inc(counts_read, 1)
                dve.wait_ge(counts_read, 2)
                chained(nc.vector.tensor_tensor_scan(all_of(upto[:]), all_of(reset[:]), all_of(total[:]), 0.0, ALU.mult, ALU.add))

            def count_tiles():
                chained(nc.vector.tensor_tensor(over[:], upto[:, :, TT - 1:TT].to_broadcast([P, E, TT]),
                                                steps[:].unsqueeze(1).to_broadcast([P, E, TT]), ALU.is_gt))
                chained(nc.vector.tensor_reduce(tiles_e[:], over[:], AX.X, ALU.add))
                chained(nc.vector.tensor_scalar(tiles_e[:], tiles_e[:], 1.0, None, ALU.max))
                chained(nc.vector.tensor_tensor_scan(end_e[:], one_e[:], tiles_e[:], float(NS), ALU.mult, ALU.add))
                nc.vector.tensor_scalar(lasti[:], end_e[:, E - 1:E], 3.0, None, ALU.add).then_inc(pad_done, 1)
                dve.wait_ge(pad_done, 3)
                chained(nc.vector.tensor_scalar(fours[:, 0:1], lasti[:], 2, None, ALU.arith_shift_right))
                chained(nc.vector.tensor_scalar(fours[:, 1:2], fours[:, 0:1], 4.0, -12.0, ALU.mult, ALU.add))

            def rank_tokens():
                chained(nc.vector.tensor_tensor(rank[:], upto[:], total[:], ALU.subtract))
                chained(nc.vector.tensor_tensor(ranki[:], rank[:], before[:], ALU.add))
                nc.vector.tensor_scalar(highi[:], ranki[:], 7, None, ALU.arith_shift_right).then_inc(pad_done, 1)
                chained(nc.vector.tensor_scalar(lowi[:], ranki[:], P - 1, None, ALU.bitwise_and))
                dve.wait_ge(pad_done, 4)
                chained(nc.vector.scalar_tensor_tensor(out=place[:], in0=lowi[:], scalar=float(NR), in1=highi[:],
                                                       op0=ALU.mult, op1=ALU.add))
                chained(nc.vector.scalar_tensor_tensor(out=first_e[:], in0=end_e[:], scalar=float(NS), in1=tiles_e[:],
                                                       op0=ALU.subtract, op1=ALU.subtract))
                chained(nc.vector.tensor_tensor(place[:], place[:], first_e[:].unsqueeze(2).to_broadcast([P, E, TT]), ALU.add))

            def match_choices():
                nc.vector.tensor_tensor(eqb[:], choice[:].unsqueeze(3).to_broadcast([P, TT, TOPK, E]),
                                        iotab[:].unsqueeze(1).unsqueeze(1).to_broadcast([P, TT, TOPK, E]), ALU.is_equal).then_inc(pad_done, 1)
                dve.wait_ge(pad_done, 5)
                nc.vector.tensor_tensor(eqb[:], eqb[:], place[:].rearrange("p e c -> p c e").unsqueeze(2).to_broadcast([P, TT, TOPK, E]),
                                        ALU.mult).then_inc(pad_done, 1)
                dve.wait_ge(pad_done, 6)

            def place_choices():
                nc.vector.tensor_reduce(posf[:], eqb[:], AX.X, ALU.add).then_inc(pad_done, 1)
                dve.wait_ge(pad_done, 7)
                nc.vector.tensor_copy(posi[:].rearrange("p (k c) -> p c k", c=TT), posf[:]).then_inc(pos_ready, 1)

            def number_experts():
                chained(nc.vector.tensor_tensor(past[:], tileno[:, 0, :].unsqueeze(2).to_broadcast([P, NT, E - 1]),
                                                end_e[:, 0:E - 1].unsqueeze(1).to_broadcast([P, NT, E - 1]), ALU.is_ge))
                chained(nc.vector.tensor_reduce(slot[:], past[:], AX.X, ALU.add))

            def fill_table():
                chained(nc.vector.tensor_tensor(slot[:], slot[:], tileno[:, 1, :], ALU.add))
                chained(nc.vector.tensor_scalar(meta[:, 0, :], slot[:], 1.0, None, ALU.add))
                chained(nc.vector.tensor_copy(sloti[:], slot[:]))
                chained(nc.vector.tensor_scalar(odd[:], sloti[:], 1, None, ALU.bitwise_and))
                chained(nc.vector.tensor_scalar(meta[:, 1, :], odd[:], float(WCOLS), None, ALU.mult))
                chained(nc.vector.tensor_tensor(fresh[:, 1:NT], slot[:, 1:NT], slot[:, 0:NT - 1], ALU.subtract))
                nc.vector.memset(fresh[:, 0:1], 0.0).then_inc(pad_done, 1)
                dve.wait_ge(pad_done, 8)
                chained(nc.vector.scalar_tensor_tensor(out=fresh[:], in0=slot[:], scalar=float(NX - 1), in1=fresh[:],
                                                       op0=ALU.is_lt, op1=ALU.mult))
                nc.vector.scalar_tensor_tensor(out=meta[:, 2, :], in0=slot[:], scalar=1.0, in1=fresh[:],
                                               op0=ALU.add, op1=ALU.mult).then_inc(meta_ready, 1)
                assert done[0] == PLAN_STEPS

            def x_low(t, s):
                dve.wait_ge(xh_done, t + 1)
                at_least(dve, up_done, t - 1)
                nc.vector.tensor_tensor(xl[:, s, :], banks[0][:], xh[:, s, :], ALU.subtract).then_inc(xl_done, 1)

            def take_weight(t, s4):
                if isinstance(t, int) and t < TT:
                    e = 1
                else:
                    e = dve.value_load(meta[0:1, 0, bass.ds(t, 1)], min_val=1, max_val=NX)
                apart(dve, gathered, 16 * (t + 1), "dve")
                at_least(dve, am_done, t - 1)
                nc.vector.tensor_copy(cc[:, s4 % 2:s4 % 2 + 1], xt[:, s4, H:H + 1] if isinstance(e, int) else xt[:, s4, bass.ds(H - 1 + e, 1)]).then_inc(cc_done, 1)

            def multiply(t, s):
                dve.wait_ge(sg_done, t + 1)
                dve.wait_ge(cc_done, t + 1)
                at_least(dve, am_turned, t - 1)
                nc.vector.scalar_tensor_tensor(out=am[:, s, 0:I], in0=sg[:, s, :], scalar=cc[:, s:s + 1],
                                               in1=banks[2 + 2 * s][:, 0:I], op0=ALU.mult, op1=ALU.mult).then_inc(am_done, 1)

            def a_low(t, s):
                dve.wait_ge(ah_done, t + 1)
                at_least(dve, down_done, t - 1)
                nc.vector.tensor_tensor(al[:, s, :], banks[5][:, 0:IP], ah[:, s, :], ALU.subtract).then_inc(al_done, 1)

            def next_weights(t):
                e = dve.value_load(meta[0:1, 2, bass.ds(t, 1)], min_val=0, max_val=NX - 1)
                with dve.If(e > 0):
                    apart(dve, raw_in, 16 * (e + 1), "dve")
                    apart(dve, down_done, t, "dve")
                    nc.vector.tensor_copy(wh[:, bass.ds((e % 2) * WCOLS + WCOLS - SHARE, SHARE)],
                                          wraw[:, WCOLS - SHARE:WCOLS]).then_inc(wh_done, 1)

            def tile(t, s4):
                s = s4 % 2
                a_low(t - 1, 1 - s)
                take_weight(t + 1, (s4 + 1) % 4)
                x_low(t + 1, 1 - s)
                multiply(t, s)

            read_counts()
            take_weight(0, 0)
            x_low(0, 0)
            take_weight(1, 1)
            x_low(1, 1)
            count_tiles()
            multiply(0, 0)
            for t, part in enumerate((rank_tokens, match_choices, place_choices, number_experts, fill_table), 1):
                tile(t, t % 4)
                part()
            tile(PEELED - 1, (PEELED - 1) % 4)
            dve.wait_ge(meta_ready, 1)
            groups = tile_groups(dve)
            with dve.Fori(1, groups - 1) as i:
                for k in range(4):
                    tile(4 * i + 3 + k, (3 + k) % 4)
                    next_weights(4 * i + 3 + k)
            last = tiles_but_12(dve) + 11
            a_low(last - 1, 0)
            multiply(last, 1)
            a_low(last, 1)

        @block.tensor
        def _(pe):
            pe.wait_ge(const_in, 16 * N_CONST)

            def claim(stage, i, q, held=False):
                bank, m = use(stage, i, q)
                if held:
                    apart(pe, gone[bank], m, "pe")
                else:
                    at_least(pe, gone[bank], m)
                return misc[bank], full[bank]

            def inproj(q, j):
                pe.wait_ge(ctx_in, 16 * (q + 1))
                bank, done = claim("inproj", j, q)
                for k in range(KC):
                    mm = nc.tensor.matmul(bank[:], inw[:, k, j * P:(j + 1) * P], ctxt[:, k, :], start=k == 0, stop=k == KC - 1)
                mm.then_inc(done, 1)

            def xproj(q, _):
                pe.wait_ge(silu_done, J * (q + 1))
                bank, done = claim("xproj", 0, q)
                for k in range(J):
                    mm = nc.tensor.matmul(bank[0:XP, :], xpw[:, k, :], u[:, bass.ds(q % 2, 1), k, :].rearrange("p a t -> p (a t)"),
                                          start=k == 0, stop=k == J - 1)
                mm.then_inc(done, 1)

            def dt(q, j):
                if j == 0:
                    xb, xm = use("xproj", 0, q)
                    pe.wait_ge(gone[xb], xm + 1)
                bank, done = claim("dt", j, q)
                nc.tensor.matmul(bank[:], dtw[:, j * P:(j + 1) * P], xd[DTP:DTP + DR, :], start=True, stop=True).then_inc(done, 1)

            def bt(q, _):
                bank, done = claim("bt", 0, q, True)
                if not (isinstance(q, int) and q == 0):
                    apart(pe, btc_done, q, "pe")
                for t in range(TC):
                    mm = nc.tensor.transpose(bank[:, t * DS:(t + 1) * DS], xd[BP:BP + DS, t * P:(t + 1) * P], ident[BP:BP + DS, BP:BP + DS])
                mm.then_inc(done, 1)

            def dut(q, j):
                pe.wait_ge(du_done, J * q + j + 1)
                bank, done = claim("dut", j, q)
                for t in range(TC):
                    mm = nc.tensor.transpose(bank[:, t * P:(t + 1) * P], du[:, j, t * P:(t + 1) * P], ident[:])
                mm.then_inc(done, 1)

            def add_product(b, n, j):
                pe.wait_ge(hc_done, (b * DS + n) * J + j + 1)
                if n == 0:
                    at_least(pe, y_done, J * (b - 1) + j + 1)
                nc.tensor.matmul(ysum[j][:], ident[:], hc[:, j, :], start=n == 0, stop=n == DS - 1,
                                 skip_group_check=True).then_inc(summed, 1)

            def step(b, n):
                before = (b, n - 1) if n else None if isinstance(b, int) and b == 0 else (b - 1, DS - 1)
                pe.wait_ge(g_done, b * DS + n + 1)
                for j in range(J):
                    at_least(pe, scanned, (b * DS + n) * J + j - 1)
                    for t in range(TC):
                        mm = nc.tensor.transpose(dbu[j % 2][:, t * P:(t + 1) * P], gt[:, n % 2, t, j * P:(j + 1) * P], ident[:])
                    mm.then_inc(turned, 1)
                    if before and j in (1, 2):
                        add_product(*before, j - 1)

            def rest(b, n):
                before = (b, n - 1) if n else None if isinstance(b, int) and b == 0 else (b - 1, DS - 1)
                if before:
                    add_product(*before, 2)
                    add_product(*before, 3)

            def tail(b, _):
                for j in range(J):
                    add_product(b, DS - 1, j)

            def skip(q, which):
                kind, i = which
                bank, m = use(kind, i, q)
                at_least(pe, gone[bank], m)
                pe.sem_inc(full[bank], 1)
                pe.sem_inc(gone[bank], 1)

            def yt(b, t):
                pe.wait_ge(yz_done, J * (b + 1))
                bank, done = claim("yt", t, b)
                for j in range(J):
                    mm = nc.tensor.transpose(bank[:, j * P:(j + 1) * P], y[:, j, t * P:(t + 1) * P], ident[:])
                mm.then_inc(done, 1)

            def xlt(b, t):
                pe.wait_ge(norm_done, TC * b + t + 1)
                bank, done = claim("xlt", t, b)
                for k in range(HK):
                    mm = nc.tensor.transpose(bank[:, k * P:(k + 1) * P], rowb[:, t, k * P:(k + 1) * P], ident[:])
                mm.then_inc(done, 1)

            def gate(b, _):
                xb, xm = use("xlt", 3, b)
                pe.wait_ge(gone[xb], xm + 1)
                bank, done = claim("gate", 0, b)
                for t in range(TC):
                    for k in range(HK):
                        mm = nc.tensor.matmul(bank[:, t * E:(t + 1) * E], xlT[:, t, k, :], gw[:, k, :],
                                              start=k == 0, stop=k == HK - 1)
                mm.then_inc(done, 1)

            stage_a(pe, PE_WORK, {"inproj": inproj, "xproj": xproj, "bt": bt, "dt": dt, "dut": dut, "step": step,
                                 "rest": rest, "yt": yt, "xlt": xlt, "gate": gate, "skip": skip},
                    after_scans=lambda: tail(NB - 1, 0))

            pe.wait_ge(rows_stored, 16 * (NB + 1))
            pe.wait_ge(sel_done, 2 * NB)
            pe.wait_ge(plan_in, 16 * N_PLAN)
            nc.tensor.matmul(banks[1][:, 0:E * TT], tri[:], sel[:].rearrange("p e c -> p (e c)"), start=True, stop=True)
            nc.tensor.matmul(banks[0][:, 0:E * TT], ones[:], sel[:].rearrange("p e c -> p (e c)"), start=True, stop=True).then_inc(counted, 1)
            pe.wait_ge(counts_read, 2)

            def turn_x(t, s):
                apart(pe, gathered, 16 * (t + 1), "pe")
                at_least(pe, xl_done, t)
                for k in range(HK):
                    mm = nc.tensor.transpose(banks[0][:, k * P:(k + 1) * P], xt[:, s, k * P:(k + 1) * P], ident[:])
                mm.then_inc(xt_turned, 1)

            def up(t, s, chunks, off):
                gate_bank, up_bank = banks[1 + 2 * s], banks[2 + 2 * s]
                if chunks[0] == 0:
                    pe.wait_ge(xl_done, t + 1)
                    at_least(pe, am_done, t - 1)
                for k in chunks:
                    high, low = xh[:, s, k * P:(k + 1) * P], xl[:, s, k * P:(k + 1) * P]
                    for n, (xx, ww) in enumerate(((high, wh), (high, wl), (low, wh))):
                        first, last = k == 0 and n == 0, k == HK - 1 and n == 2
                        nc.tensor.matmul(gate_bank[:, 0:I], xx, columns(ww, off + k * 2 * I, I), start=first, stop=last)
                        mm = nc.tensor.matmul(up_bank[:, 0:I], xx, columns(ww, off + k * 2 * I + I, I), start=first, stop=last)
                if chunks[-1] == HK - 1:
                    mm.then_inc(up_done, 1)

            def turn_a(t, s):
                pe.wait_ge(am_done, t + 1)
                at_least(pe, al_done, t)
                for k in range(IK):
                    mm = nc.tensor.transpose(banks[5][:, k * P:(k + 1) * P], am[:, s, k * P:(k + 1) * P], ident[:])
                mm.then_inc(am_turned, 1)

            def columns(w, start, size):
                return w[:, start:start + size] if isinstance(start, int) else w[:, bass.ds(start, size)]

            def down(t, s, off):
                pe.wait_ge(al_done, t + 1)
                at_least(pe, ys_done, t - 1)
                for k in range(IK):
                    high, low = ah[:, s, k * P:(k + 1) * P], al[:, s, k * P:(k + 1) * P]
                    for n, (aa, ww) in enumerate(((high, wh), (high, wl), (low, wh))):
                        mm = nc.tensor.matmul(banks[6 + s][:], aa, columns(ww, off + W2AT + k * H, H),
                                              start=k == 0 and n == 0, stop=k == IK - 1 and n == 2)
                mm.then_inc(down_done, 1)

            def weights_of(t):
                needed = pe.value_load(meta[0:1, 0, bass.ds(t, 1)], min_val=1, max_val=NX)
                apart(pe, wl_done, needed, "pe")
                return pe.value_load(meta[0:1, 1, bass.ds(t, 1)], min_val=0, max_val=WCOLS)

            def tile(t, s4, old, off, more=True):
                s = s4 % 2
                up(t, s, (0, 1), off)
                turn_a(t - 1, 1 - s)
                up(t, s, (2, 3), off)
                if more:
                    turn_x(t + 1, (s4 + 1) % 4)
                down(t - 1, 1 - s, old() if callable(old) else old)

            turn_x(0, 0)
            turn_x(1, 1)
            pe.wait_ge(wl_done, 1)
            up(0, 0, (0, 1, 2, 3), 0)
            for t in range(1, PEELED):
                tile(t, t % 4, 0, 0)
            pe.wait_ge(meta_ready, 1)
            groups = tile_groups(pe)
            with pe.Fori(1, groups - 1) as i:
                def old():
                    return pe.value_load(meta[0:1, 1, bass.ds(4 * i + 2, 1)], min_val=0, max_val=WCOLS)

                for k in range(4):
                    off = weights_of(4 * i + 3 + k)
                    tile(4 * i + 3 + k, (3 + k) % 4, old, off)
                    old = off
            last = tiles_but_12(pe) + 11

            def of_last(k):
                return pe.value_load(meta[0:1, 1, bass.ds(last - k, 1)], min_val=0, max_val=WCOLS)

            tile(last, 3, lambda: of_last(1), weights_of(last), False)
            turn_a(last, 1)
            down(last, 1, of_last(0))


def kernel(**inputs):
    import numpy as np
    import concourse.bacc as bacc
    from concourse.bass_utils import run_bass_kernel_spmd

    a = {k: np.asarray(v) for k, v in inputs.items()}
    f = a["x"].dtype
    xp = a["L0_xattn_x_proj_w"]
    xpT = np.zeros((DI, XP), f)
    xpT[:, DTP:DTP + DR] = xp[:DR].T
    xpT[:, BP:BP + DS] = xp[DR:DR + DS].T
    xpT[:, CP:CP + DS] = xp[DR + DS:].T
    s13, s2 = a["L0_ffn_sw13"], a["L0_ffn_sw2"]
    w13 = np.concatenate([np.stack([np.concatenate([s13[I * i:I * i + I], s13[2 * I + I * i:3 * I + I * i]]) for i in range(2)]), a["L0_ffn_w13"]])
    w2 = np.concatenate([np.stack([s2[:, I * i:I * i + I] for i in range(2)]), a["L0_ffn_w2"]])
    wall = np.zeros((NX, P, WCOLS), f)
    wall[:, :, :W2AT] = w13.transpose(0, 2, 1).reshape(NX, HK, P, 2 * I).transpose(0, 2, 1, 3).reshape(NX, P, W2AT)
    w2p = np.zeros((NX, IP, H), f)
    w2p[:, :I] = w2.transpose(0, 2, 1)
    wall[:, :, W2AT:] = w2p.reshape(NX, IK, P, H).transpose(0, 2, 1, 3).reshape(NX, P, IK * H)
    part, tiles = np.arange(P, dtype=np.int32)[:, None], np.arange(NT)
    reset = np.ones((P, E, TT), np.float32)
    reset[:, :, 0] = 0
    number = np.stack([tiles, np.minimum(tiles // TT, 2)]).astype(np.float32)
    arrays = {
        "x": a["x"], "ctxT": a["ctx_1024"].transpose(0, 2, 1), "g_x": a["g_xattn"], "g_f": a["g_ffn"],
        "inT": a["L0_xattn_in_proj_w"].T, "convw": a["L0_xattn_conv_w"], "convb": a["L0_xattn_conv_b"],
        "xpT": xpT, "dtwT": a["L0_xattn_dt_proj_w"].T, "dtb": a["L0_xattn_dt_proj_b"],
        "alog": a["L0_xattn_A_log"], "dvec": a["L0_xattn_D"], "gateT": a["L0_ffn_gate_w"].T, "wall": wall,
        "ident_d": np.eye(P, dtype=np.float32), "iota_d": np.tile(np.arange(DS, dtype=np.float32), (P, 1)),
        "tri_d": np.triu(np.ones((P, P), np.float32), 1), "ones_d": np.ones((P, P), np.float32), "reset_d": reset,
        "steps_d": np.tile(np.arange(TT, dtype=np.float32) * P, (P, 1)), "tile_d": np.tile(number, (P, 1, 1)),
        "ids_d": np.int32(P) * (np.arange(NS, dtype=np.int32) % TT) + part, "trash_d": TOKENS + part + np.zeros((P, NR), np.int32),
    }
    arrays = {f"in_{k}": np.ascontiguousarray(v) for k, v in arrays.items()}
    nc = bacc.Bacc("TRN2", target_bir_lowering=False, num_devices=1)
    args = [nc.dram_tensor(k, v.shape, mybir.dt.from_np(v.dtype), kind="ExternalInput").ap() for k, v in arrays.items()]
    out = nc.dram_tensor("out_x", (NB, L, H), F32, kind="ExternalOutput").ap()
    mamba_moe(nc, *args, out)
    r = run_bass_kernel_spmd(nc, [arrays], core_ids=[0])
    return r.results[0]["out_x"]
```
